# Optimizing a Trainium2 kernel written in Bass

```python
import numpy as np
import jax
import jax.numpy as jnp

def _softmax(x, axis=-1):
    return jax.nn.softmax(x, axis=axis)

def _gelu(x):
    return jax.nn.gelu(x, approximate=True)

def _silu(x):
    return jax.nn.silu(x)

def _sigmoid(x):
    return jax.nn.sigmoid(x)

def _layernorm(x, axis=-1, eps=1e-05):
    m = jnp.mean(x, axis=axis, keepdims=True)
    v = jnp.var(x, axis=axis, keepdims=True)
    return (x - m) / jnp.sqrt(v + eps)

def _scatter_add(tgt, idx, src, axis=0):
    return tgt.at[idx].add(src)

def _segment_sum(src, seg, n):
    return jax.ops.segment_sum(src, seg, n)
kernel_name = 'mk_gnn_resnorm_d4_gnn_r16_be3747'

def setup_inputs(seed: int=0):
    np.random.seed(seed)
    _w = jnp.asarray

    def _rec_inputs():
        import jax
        import jax.numpy as jnp
        _gk = jax.random.key(seed)
        x = -0.0005121 + 1.001 * jax.random.normal(jax.random.fold_in(_gk, 1), (3125, 64), jnp.float32)
        src = jax.random.randint(jax.random.fold_in(_gk, 2), (100000,), 0, 3125, jnp.int32)
        dst = jax.random.randint(jax.random.fold_in(_gk, 3), (100000,), 0, 3125, jnp.int32)
        _o = jnp.argsort(dst, stable=True)
        src = src[_o]
        dst = dst[_o]
        edge_attr_64 = -9.77346e-05 + 0.999888 * jax.random.normal(jax.random.fold_in(_gk, 13), (100000, 64), jnp.float32)
        edge_type_8 = jax.random.randint(jax.random.fold_in(_gk, 15), (100000,), 0, 8, jnp.int32)
        edge_weight = 0.000452788 + 0.999756 * jax.random.normal(jax.random.fold_in(_gk, 16), (100000,), jnp.float32)
        return (x, src, dst, edge_attr_64, edge_type_8, edge_weight)
    x, src, dst, edge_attr_64, edge_type_8, edge_weight = _rec_inputs()

    def _L0_gnn_setup():
        import jax, jax.numpy as jnp
        import numpy as np
        N_NODES = 3125
        N_EDGES = 50000
        D = 64
        LEAKY_SLOPE = 0.01

        def gat_layer(h, src, dst, W, b, aW, ab):
            z = h @ W.T + b
            zs = z[src]
            zd = z[dst]
            e = jnp.concatenate([zs, zd], axis=-1) @ aW.T + ab
            e = jax.nn.leaky_relu(e, LEAKY_SLOPE)[:, 0]
            m = jax.ops.segment_max(e, dst, num_segments=N_NODES)
            ex = jnp.exp(e - m[dst])
            den = jax.ops.segment_sum(ex, dst, num_segments=N_NODES)
            alpha = ex / den[dst]
            return jax.ops.segment_sum(alpha[:, None] * zs, dst, num_segments=N_NODES)
        key = jax.random.key(seed)
        ks = jax.random.split(key, 16)
        x = jax.random.normal(ks[0], (N_NODES, D), dtype=jnp.float32)
        src = jax.random.randint(ks[1], (N_EDGES,), 0, N_NODES)
        dst = jax.random.randint(ks[2], (N_EDGES,), 0, N_NODES)
        gain = float(np.sqrt(2.0))
        params = {}
        for i in range(3):
            std_fc = gain * np.sqrt(2.0 / (D + D))
            std_at = gain * np.sqrt(2.0 / (2 * D + 1))
            params[f'W{i}'] = jax.random.normal(ks[3 + 4 * i], (D, D), dtype=jnp.float32) * std_fc
            params[f'b{i}'] = jnp.zeros((D,), dtype=jnp.float32)
            params[f'a{i}'] = jax.random.normal(ks[4 + 4 * i], (1, 2 * D), dtype=jnp.float32) * std_at
            params[f'ab{i}'] = jnp.zeros((1,), dtype=jnp.float32)
        return {'x': x, 'src': src, 'dst': dst, **params}
    _L0_gnn_all = _L0_gnn_setup()
    _L0_gnn_in = {k: v for k, v in _L0_gnn_all.items() if k in ('W0', 'b0', 'a0', 'ab0', 'W1', 'b1', 'a1', 'ab1', 'W2', 'b2', 'a2', 'ab2')}
    del _L0_gnn_all

    def _L1_gnn_setup():
        import jax, jax.numpy as jnp
        import numpy as np
        N_NODES = 3125
        N_EDGES = 50000
        N_GRAPHS = 16
        D = 64
        H = 128
        key = jax.random.key(seed)
        ks = jax.random.split(key, 12)
        s = lambda fan_in: 1.0 / np.sqrt(fan_in)
        inp = {'x': jax.random.normal(ks[0], (N_NODES, D), jnp.float32), 'edge_attr': jax.random.normal(ks[1], (N_EDGES, D), jnp.float32), 'u': jax.random.normal(ks[2], (N_GRAPHS, D), jnp.float32), 'W1a': jax.random.normal(ks[3], (2 * D, H), jnp.float32) * s(2 * D), 'b1a': jnp.zeros((H,), jnp.float32), 'W1b': jax.random.normal(ks[4], (H, D), jnp.float32) * s(H), 'b1b': jnp.zeros((D,), jnp.float32), 'W2a': jax.random.normal(ks[5], (3 * D, H), jnp.float32) * s(3 * D), 'b2a': jnp.zeros((H,), jnp.float32), 'W2b': jax.random.normal(ks[6], (H, D), jnp.float32) * s(H), 'b2b': jnp.zeros((D,), jnp.float32), 'edge_index': jax.random.randint(ks[7], (2, N_EDGES), 0, N_NODES, jnp.int64), 'batch': jnp.sort(jax.random.randint(ks[8], (N_NODES,), 0, N_GRAPHS, jnp.int64))}
        return inp
    _L1_gnn_all = _L1_gnn_setup()
    _L1_gnn_in = {k: v for k, v in _L1_gnn_all.items() if k in ('u', 'W1a', 'b1a', 'W1b', 'b1b', 'W2a', 'b2a', 'W2b', 'b2b')}
    del _L1_gnn_all

    def _L2_gnn_setup():
        import jax, jax.numpy as jnp
        import numpy as np
        N_NODES = 6250
        N_EDGES = 75000
        D_IN = 64
        D_OUT = 64
        N_REL = 8
        key = jax.random.key(seed)
        k1, k2, k3, k4, k5 = jax.random.split(key, 5)
        x = jax.random.normal(k1, (N_NODES, D_IN), dtype=jnp.float32)
        edge_index = jax.random.randint(k2, (2, N_EDGES), 0, N_NODES, dtype=jnp.int32)
        edge_type = jax.random.randint(k3, (N_EDGES,), 0, N_REL, dtype=jnp.int32)
        wb = float(np.sqrt(6.0 / (D_IN + D_OUT)))
        weight = jax.random.uniform(k4, (N_REL, D_IN, D_OUT), dtype=jnp.float32, minval=-wb, maxval=wb)
        self_loop_w = jax.random.uniform(k5, (D_OUT, D_IN), dtype=jnp.float32, minval=-wb, maxval=wb)
        return {'x': x, 'edge_index': edge_index, 'edge_type': edge_type, 'weight': weight, 'self_loop_w': self_loop_w}
    _L2_gnn_all = _L2_gnn_setup()
    _L2_gnn_in = {k: v for k, v in _L2_gnn_all.items() if k in ('weight', 'self_loop_w')}
    del _L2_gnn_all

    def _L3_gnn_setup():
        import jax, jax.numpy as jnp
        import numpy as np
        N = 6250
        E = 100000
        IN, H, OUT = (64, 128, 64)

        def _gcn(x, src, tgt, w, W, b, n):
            h = x @ W.T
            deg = jax.ops.segment_sum(w, tgt, num_segments=n) + 1.0
            dinv = jnp.where(deg > 0, jax.lax.rsqrt(deg), 0.0)
            norm = dinv[src] * w * dinv[tgt]
            agg = jax.ops.segment_sum(h[src] * norm[:, None], tgt, num_segments=n)
            return agg + h * (dinv * dinv)[:, None] + b
        key = jax.random.key(seed)
        ks = jax.random.split(key, 12)

        def lin(k, o, i):
            return jax.random.normal(k, (o, i), dtype=jnp.float32) / np.sqrt(i)
        return {'x': jax.random.normal(ks[0], (N, IN), dtype=jnp.float32), 'edge_index': jax.random.randint(ks[1], (2, E), 0, N), 'edge_weight': jax.random.normal(ks[2], (E,), dtype=jnp.float32), 'W1p': lin(ks[3], H, IN), 'b1p': jnp.zeros((H,), jnp.float32), 'W1n': lin(ks[4], H, IN), 'b1n': jnp.zeros((H,), jnp.float32), 'W2p': lin(ks[5], OUT, H), 'b2p': jnp.zeros((OUT,), jnp.float32), 'W2n': lin(ks[6], OUT, H), 'b2n': jnp.zeros((OUT,), jnp.float32)}
    _L3_gnn_all = _L3_gnn_setup()
    _L3_gnn_in = {k: v for k, v in _L3_gnn_all.items() if k in ('W1p', 'b1p', 'W1n', 'b1n', 'W2p', 'b2p', 'W2n', 'b2n')}
    del _L3_gnn_all
    return {'x': x, 'src': src, 'dst': dst, 'edge_attr_64': edge_attr_64, 'edge_type_8': edge_type_8, 'edge_weight': edge_weight, 'L0_gnn_W0': _L0_gnn_in['W0'], 'L0_gnn_b0': _L0_gnn_in['b0'], 'L0_gnn_a0': _L0_gnn_in['a0'], 'L0_gnn_ab0': _L0_gnn_in['ab0'], 'L0_gnn_W1': _L0_gnn_in['W1'], 'L0_gnn_b1': _L0_gnn_in['b1'], 'L0_gnn_a1': _L0_gnn_in['a1'], 'L0_gnn_ab1': _L0_gnn_in['ab1'], 'L0_gnn_W2': _L0_gnn_in['W2'], 'L0_gnn_b2': _L0_gnn_in['b2'], 'L0_gnn_a2': _L0_gnn_in['a2'], 'L0_gnn_ab2': _L0_gnn_in['ab2'], 'L1_gnn_u': _L1_gnn_in['u'], 'L1_gnn_W1a': _L1_gnn_in['W1a'], 'L1_gnn_b1a': _L1_gnn_in['b1a'], 'L1_gnn_W1b': _L1_gnn_in['W1b'], 'L1_gnn_b1b': _L1_gnn_in['b1b'], 'L1_gnn_W2a': _L1_gnn_in['W2a'], 'L1_gnn_b2a': _L1_gnn_in['b2a'], 'L1_gnn_W2b': _L1_gnn_in['W2b'], 'L1_gnn_b2b': _L1_gnn_in['b2b'], 'L2_gnn_weight': _L2_gnn_in['weight'], 'L2_gnn_self_loop_w': _L2_gnn_in['self_loop_w'], 'L3_gnn_W1p': _L3_gnn_in['W1p'], 'L3_gnn_b1p': _L3_gnn_in['b1p'], 'L3_gnn_W1n': _L3_gnn_in['W1n'], 'L3_gnn_b1n': _L3_gnn_in['b1n'], 'L3_gnn_W2p': _L3_gnn_in['W2p'], 'L3_gnn_b2p': _L3_gnn_in['b2p'], 'L3_gnn_W2n': _L3_gnn_in['W2n'], 'L3_gnn_b2n': _L3_gnn_in['b2n']}

def reference(x, src, dst, edge_attr_64, edge_type_8, edge_weight, L0_gnn_W0, L0_gnn_b0, L0_gnn_a0, L0_gnn_ab0, L0_gnn_W1, L0_gnn_b1, L0_gnn_a1, L0_gnn_ab1, L0_gnn_W2, L0_gnn_b2, L0_gnn_a2, L0_gnn_ab2, L1_gnn_u, L1_gnn_W1a, L1_gnn_b1a, L1_gnn_W1b, L1_gnn_b1b, L1_gnn_W2a, L1_gnn_b2a, L1_gnn_W2b, L1_gnn_b2b, L2_gnn_weight, L2_gnn_self_loop_w, L3_gnn_W1p, L3_gnn_b1p, L3_gnn_W1n, L3_gnn_b1n, L3_gnn_W2p, L3_gnn_b2p, L3_gnn_W2n, L3_gnn_b2n):
    import jax
    import jax.numpy as jnp

    def _L0_gnn_ref(x, src, dst, W0, b0, a0, ab0, W1, b1, a1, ab1, W2, b2, a2, ab2):
        import jax, jax.numpy as jnp
        import numpy as np
        N_NODES = 3125
        N_EDGES = 50000
        D = 64
        LEAKY_SLOPE = 0.01

        def gat_layer(h, src, dst, W, b, aW, ab):
            z = h @ W.T + b
            zs = z[src]
            zd = z[dst]
            e = jnp.concatenate([zs, zd], axis=-1) @ aW.T + ab
            e = jax.nn.leaky_relu(e, LEAKY_SLOPE)[:, 0]
            m = jax.ops.segment_max(e, dst, num_segments=N_NODES)
            ex = jnp.exp(e - m[dst])
            den = jax.ops.segment_sum(ex, dst, num_segments=N_NODES)
            alpha = ex / den[dst]
            return jax.ops.segment_sum(alpha[:, None] * zs, dst, num_segments=N_NODES)
        h = gat_layer(x, src, dst, W0, b0, a0, ab0)
        h = jax.nn.relu(h)
        h = gat_layer(h, src, dst, W1, b1, a1, ab1)
        h = jax.nn.relu(h)
        h = gat_layer(h, src, dst, W2, b2, a2, ab2)
        return h

    def _L1_gnn_ref(x, edge_attr, u, W1a, b1a, W1b, b1b, W2a, b2a, W2b, b2b, edge_index, batch):
        import jax, jax.numpy as jnp
        import numpy as np
        N_NODES = 3125
        N_EDGES = 50000
        N_GRAPHS = 16
        D = 64
        H = 128
        row, col = (edge_index[0], edge_index[1])
        h = jnp.concatenate([x[row], edge_attr], axis=1)
        h = jnp.maximum(h @ W1a + b1a, 0.0) @ W1b + b1b
        ssum = jax.ops.segment_sum(h, col, num_segments=x.shape[0])
        cnt = jax.ops.segment_sum(jnp.ones((h.shape[0], 1), h.dtype), col, num_segments=x.shape[0])
        mean = jnp.where(cnt > 0, ssum / jnp.maximum(cnt, 1.0), 0.0)
        z = jnp.concatenate([x, mean, u[batch]], axis=1)
        return jnp.maximum(z @ W2a + b2a, 0.0) @ W2b + b2b

    def _L2_gnn_ref(x, edge_index, edge_type, weight, self_loop_w):
        import jax, jax.numpy as jnp
        import numpy as np
        N_NODES = 6250
        N_EDGES = 75000
        D_IN = 64
        D_OUT = 64
        N_REL = 8
        num_nodes = x.shape[0]
        num_relations = weight.shape[0]
        src, dst = (edge_index[0], edge_index[1])
        x_src = x[src]
        out = jnp.zeros((num_nodes, weight.shape[2]), dtype=x.dtype)
        for r in range(num_relations):
            mask = (edge_type == r)[:, None]
            msg = jnp.where(mask, x_src @ weight[r], 0.0)
            out = out + jax.ops.segment_sum(msg, dst, num_segments=num_nodes)
        out = out + x @ self_loop_w.T
        return jax.nn.relu(out)

    def _L3_gnn_ref(x, edge_index, edge_weight, W1p, b1p, W1n, b1n, W2p, b2p, W2n, b2n):
        import jax, jax.numpy as jnp
        import numpy as np
        N = 6250
        E = 100000
        IN, H, OUT = (64, 128, 64)

        def _gcn(x, src, tgt, w, W, b, n):
            h = x @ W.T
            deg = jax.ops.segment_sum(w, tgt, num_segments=n) + 1.0
            dinv = jnp.where(deg > 0, jax.lax.rsqrt(deg), 0.0)
            norm = dinv[src] * w * dinv[tgt]
            agg = jax.ops.segment_sum(h[src] * norm[:, None], tgt, num_segments=n)
            return agg + h * (dinv * dinv)[:, None] + b
        src, tgt = (edge_index[0], edge_index[1])
        n = x.shape[0]
        wp = jnp.where(edge_weight >= 0, edge_weight, 0.0)
        wn = jnp.where(edge_weight < 0, -edge_weight, 0.0)
        h = jax.nn.relu(_gcn(x, src, tgt, wp, W1p, b1p, n) - _gcn(x, src, tgt, wn, W1n, b1n, n))
        out = jax.nn.relu(_gcn(h, src, tgt, wp, W2p, b2p, n) - _gcn(h, src, tgt, wn, W2n, b2n, n))
        return out
    edge_index = jnp.stack([src, dst])
    batch0 = jnp.zeros((3125,), jnp.int32)
    x = _layernorm(x + _L0_gnn_ref(x, src, dst, L0_gnn_W0, L0_gnn_b0, L0_gnn_a0, L0_gnn_ab0, L0_gnn_W1, L0_gnn_b1, L0_gnn_a1, L0_gnn_ab1, L0_gnn_W2, L0_gnn_b2, L0_gnn_a2, L0_gnn_ab2), axis=-1)
    x = _layernorm(x + _L1_gnn_ref(x, edge_attr_64, L1_gnn_u, L1_gnn_W1a, L1_gnn_b1a, L1_gnn_W1b, L1_gnn_b1b, L1_gnn_W2a, L1_gnn_b2a, L1_gnn_W2b, L1_gnn_b2b, edge_index, batch0), axis=-1)
    x = _layernorm(x + _L2_gnn_ref(x, edge_index, edge_type_8, L2_gnn_weight, L2_gnn_self_loop_w), axis=-1)
    x = _layernorm(x + _L3_gnn_ref(x, edge_index, edge_weight, L3_gnn_W1p, L3_gnn_b1p, L3_gnn_W1n, L3_gnn_b1n, L3_gnn_W2p, L3_gnn_b2p, L3_gnn_W2n, L3_gnn_b2n), axis=-1)
    return x

_drawn_inputs = setup_inputs


def setup_inputs(seed=0):
    import zlib

    import numpy as np

    out = dict(_drawn_inputs(seed))
    spreads = {'L0_gnn_b0': (0.0, 0.1),
     'L0_gnn_b1': (0.0, 0.1),
     'L0_gnn_b2': (0.0, 0.1),
     'L1_gnn_b1a': (0.0, 0.285),
     'L1_gnn_b1b': (0.0, 0.1),
     'L1_gnn_b2a': (0.0, 0.1),
     'L1_gnn_b2b': (0.0, 0.1),
     'L3_gnn_b1p': (0.0, 0.1),
     'L3_gnn_b1n': (0.0, 0.1),
     'L3_gnn_b2p': (0.0, 0.1),
     'L3_gnn_b2n': (0.0, 0.1)}
    factors = {'edge_attr_64': 2.922, 'L0_gnn_a2': 4.145}
    for name, (base, spread) in spreads.items():
        noise = np.random.default_rng([zlib.crc32(name.encode()), seed]).standard_normal(out[name].shape)
        drawn = base * np.exp(spread * noise) if base else spread * noise
        out[name] = jnp.asarray(drawn.astype(out[name].dtype))
    for name, factor in factors.items():
        out[name] = (out[name] * factor).astype(out[name].dtype)
    return out
```

```python
import concourse.bass as bass
from concourse import mybir
from contextlib import ExitStack, contextmanager

FP32 = mybir.dt.float32
INT32 = mybir.dt.int32
ALU = mybir.AluOpType
ACT = mybir.ActivationFunctionType
AX = mybir.AxisListType

P = 128
N = 3125
E = 100000
D = 64
H = 128
RELS = 8
NT = -(-N // P)
NPAD = NT * P
G = 14
SLOTS = 4
NG = -(-E // (P * G * SLOTS)) * SLOTS
ET = NG * G
EPAD = ET * P
AHEAD = 2
CH = 4
CHUNKS = [(c, min(c + CH, G)) for c in range(0, G, CH)]
NC = len(CHUNKS)
NB = 5
NSTEP = NT // NB
GATHERED = 16 * G
SLOPE = 0.01
EPS = 1e-5
ZROW = D + 2
HROW = H + 3


WEIGHTS = [(f"W0{l}", D, D) for l in range(3)] + [(f"b_0{l}", P, D) for l in range(3)]
WEIGHTS += [(f"a_src{l}", P, D) for l in range(3)] + [(f"a_dst{l}", P, D) for l in range(3)]
WEIGHTS += [(f"b_att{l}", P, 1) for l in range(3)]
WEIGHTS += [
    ("W1a_node", D, H), ("W1a_edge", D, H), ("b_1a", P, H), ("W1b", H, D), ("b_1b", P, D),
    ("W2a", 2 * D, H), ("W2a_u", D, H), ("c_u", D, 1), ("c_2a", H, 1), ("W2b", H, D), ("b_2b", P, D),
    ("Wrel", D, RELS * D), ("Wself", D, D),
    ("W3a", 2 * D, H), ("c_3p", H, 1), ("c_3n", H, 1), ("W3b", H, 2 * D), ("b_3p", P, D), ("b_3n", P, D),
]


def weight_sources(d):
    row = lambda a: a.partition_broadcast(P)
    column = lambda a: a.rearrange("(n o) -> n o", o=1)
    at = {}
    for l in range(3):
        at[f"W0{l}"] = d[f"L0_gnn_W{l}"]
        at[f"b_0{l}"] = row(d[f"L0_gnn_b{l}"])
        at[f"a_src{l}"] = row(d[f"L0_gnn_a{l}"][0, :])
        at[f"a_dst{l}"] = row(d[f"L0_gnn_a{l}"][1, :])
        at[f"b_att{l}"] = row(d[f"L0_gnn_ab{l}"])
    at.update({
        "W1a_node": d["L1_gnn_W1a"][0:D, :], "W1a_edge": d["L1_gnn_W1a"][D:2 * D, :], "b_1a": row(d["L1_gnn_b1a"]),
        "W1b": d["L1_gnn_W1b"], "b_1b": row(d["L1_gnn_b1b"]), "W2a": d["L1_gnn_W2a"][0:2 * D, :],
        "W2a_u": d["L1_gnn_W2a"][2 * D:3 * D, :], "c_u": column(d["L1_gnn_u"][0, :]),
        "c_2a": column(d["L1_gnn_b2a"]), "W2b": d["L1_gnn_W2b"], "b_2b": row(d["L1_gnn_b2b"]),
        "Wrel": d["L2_gnn_weight"], "Wself": d["L2_gnn_self_loop_w"],
        "W3a": d["L3_gnn_W1"], "c_3p": column(d["L3_gnn_b1p"]), "c_3n": column(d["L3_gnn_b1n"]),
        "W3b": d["L3_gnn_W2"], "b_3p": row(d["L3_gnn_b2p"]), "b_3n": row(d["L3_gnn_b2n"]),
    })
    return at


@contextmanager
def semaphores(nc, tag):
    held = []

    def sem(name):
        held.append(nc.alloc_semaphore(f"{tag}_{name}"))
        return held[-1]

    yield sem
    nc.clear_and_free_semaphores(held)
    nc.all_engine_barrier()


class Chain:

    def __init__(self, eng, sem):
        self.eng, self.sem, self.n = eng, sem, 0

    def link(self, ins):
        self.n += 1
        ins.then_inc(self.sem, 1)
        self.eng.wait_ge(self.sem, self.n)


class Program:
    def __init__(self, nc, ctx, dram):
        self.nc, self.ctx, self.dram = nc, ctx, dram
        sb = self.sb
        self.x = sb("x", [P, NT, D])
        self.h = sb("h", [P, NT, D])
        self.acc = sb("acc", [P, NT, HROW])
        self.ident = sb("ident", [P, P])
        self.iota = sb("iota", [P, P])
        self.tile_base = sb("tile_base", [P, NT])
        self.src_idx = sb("src_idx", [P, ET + AHEAD * G], INT32)
        self.rel_idx = sb("rel_idx", [P, ET + AHEAD * G], INT32)
        self.sign_idx = sb("sign_idx", [P, ET + AHEAD * G], INT32)
        self.dst_f = sb("dst_f", [P, ET])
        self.wpos = sb("wpos", [P, ET])
        self.wneg = sb("wneg", [P, ET])
        self.bounds = sb("bounds", [1, 3 * NG], INT32)
        self.dinv = sb("dinv", [P, NT, 2])
        self.rows = sb("rows", [P, SLOTS, G, H])
        self.stage_idx = sb("stage_idx", [P, SLOTS, G], INT32)
        self.hot = sb("hot", [P, G, P])
        self.edge_a = sb("edge_a", [P, G, HROW])
        self.edge_b = sb("edge_b", [P, G, P])
        self.dst_rel = sb("dst_rel", [P, G])
        self.table = sb("table", [P, NT, H])
        self.wide_table = sb("wide_table", [P, NB, RELS * D])
        self.node_in = sb("node_in", [P, NB, H])
        self.node_inT = sb("node_inT", [P, NB * P])
        self.node_midT = sb("node_midT", [P, NB * P])
        self.big = sb("big", [P, NT, H])
        self.z = sb("z", [P, NT, ZROW])
        self.s_best = sb("s_best", [P, NT])
        self.e_best = sb("e_best", [P, NT])
        self.d_low = sb("d_low", [P, NT])
        self.per_node = sb("per_node", [P, 4, NT])
        self.var = sb("var", [P, NT, 2])
        self.std = sb("std", [P, NT, 2])
        self.ones = sb("ones", [P, P])
        self.weight = {}
        for name, rows, cols in WEIGHTS:
            self.weight[name] = sb("w_" + name, [rows, cols])
        self.psum = ctx.enter_context(nc.psum_tensor("psum", [P, 8, 512], FP32))

    def sb(self, name, shape, dtype=FP32):
        return self.ctx.enter_context(self.nc.sbuf_tensor(name, shape, dtype))

    def psum_cols(self, first_bank, parts, cols):
        flat = self.psum[:, :, :].rearrange("p b c -> p (b c)")
        return flat[0:parts, 512 * first_bank:512 * first_bank + cols]


def group_bounds(eng, k, g):
    first = eng.value_load(k.bounds[0:1, bass.ds(g, 1)], min_val=0, max_val=NT - 1)
    count = eng.value_load(k.bounds[0:1, bass.ds(g + NG, 1)], min_val=1, max_val=NT)
    before = eng.value_load(k.bounds[0:1, bass.ds(g + 2 * NG, 1)], min_val=0, max_val=NT * NG)
    return first, count, before


def setup(k):
    nc, d = k.nc, k.dram
    with ExitStack() as ctx, semaphores(nc, "su") as sem:
        sb = lambda name, shape, dt=FP32: ctx.enter_context(nc.sbuf_tensor(name, shape, dt))
        weights = sem("weights")
        loaded, made, folded = sem("loaded"), sem("made"), sem("folded")
        turned, pool_step, dve_step = sem("turned"), sem("pool"), sem("dve")
        dst_i, type_i, w = sb("su_dst", [P, ET], INT32), sb("su_type", [P, ET], INT32), sb("su_w", [P, ET])
        tile_i, tile_f = sb("su_tile_i", [P, ET], INT32), sb("su_tile_f", [P, ET])
        ends, fold, row = sb("su_ends", [P, 2 * NG]), sb("su_fold", [2 * NG, 1]), sb("su_row", [1, 2 * NG])
        ones, counts = sb("su_ones", [1, NG]), sb("su_counts", [1, 3 * NG])
        neg_f = sb("su_neg_f", [P, ET])
        src_f, t_f = sb("su_src_f", [P, ET]), sb("su_t_f", [P, ET])
        int_iota, int_base = sb("su_iota", [P, P], INT32), sb("su_base", [P, NT], INT32)
        ps_ends = k.psum_cols(0, 2 * NG, P)
        ps_row = k.psum_cols(1, 1, 2 * NG)

        with nc.Block() as block:
            @block.sync
            def _(sp):
                sp.dma_start(k.x[:, :, :], d["x"].rearrange("(t p) f -> p t f", p=P)).then_inc(loaded, 16)
                sp.dma_start(k.src_idx[:, 0:ET], d["src"]).then_inc(loaded, 16)
                sp.dma_start(dst_i[:, :], d["dst"]).then_inc(loaded, 16)
                sp.dma_start(type_i[:, :], d["edge_type_8"]).then_inc(loaded, 16)
                sp.dma_start(w[:, :], d["edge_weight"]).then_inc(loaded, 16)
                for name, source in weight_sources(d).items():
                    sp.dma_start(k.weight[name][:, :], source).then_inc(weights, 16)
                sp.wait_ge(weights, 16 * len(WEIGHTS))

            @block.gpsimd
            def _(pool):
                nc.gpsimd.memset(k.ident[:, :], 0.0).then_inc(pool_step, 1)
                nc.gpsimd.iota(int_iota[:, :], pattern=[[1, P]], base=0, channel_multiplier=0).then_inc(made, 1)
                nc.gpsimd.iota(int_base[:, :], pattern=[[P, NT]], base=0, channel_multiplier=0).then_inc(made, 1)
                for idx in (k.src_idx, k.rel_idx, k.sign_idx):
                    nc.gpsimd.memset(idx[:, ET:], 0)
                pool.wait_ge(pool_step, 1)
                nc.gpsimd.affine_select(out=k.ident[:, :], in_=k.ident[:, :], compare_op=ALU.not_equal,
                                        fill=1.0, base=0, pattern=[[-1, P]], channel_multiplier=1).then_inc(made, 1)

            @block.vector
            def _(dve):
                v, chain = nc.vector, Chain(dve, dve_step)
                v.memset(ones[:, :], 1.0)
                v.memset(k.ones[:, :], 1.0)
                dve.wait_ge(loaded, 5 * 16)
                chain.link(v.tensor_scalar(tile_i[:, :], dst_i[:, :], 7, None, ALU.arith_shift_right))
                chain.link(v.tensor_copy(tile_f[:, :], tile_i[:, :]))
                per_group = tile_f[:, :].rearrange("p (g t) -> p g t", t=G)
                v.tensor_reduce(ends[:, 0:NG], per_group, AX.X, ALU.max)
                chain.link(v.tensor_reduce(ends[:, NG:], per_group, AX.X, ALU.min))
                chain.link(v.tensor_scalar(ends[:, NG:], ends[:, NG:], -1.0, None, ALU.mult))
                v.tensor_copy(k.dst_f[:, :], dst_i[:, :])
                v.tensor_copy(src_f[:, :], k.src_idx[:, 0:ET])
                chain.link(v.tensor_copy(t_f[:, :], type_i[:, :]))
                v.scalar_tensor_tensor(k.rel_idx[:, 0:ET], src_f[:, :], float(RELS), t_f[:, :], ALU.mult, ALU.add)
                v.tensor_scalar(k.wpos[:, :], w[:, :], 0.0, None, ALU.max)
                v.tensor_scalar(k.wneg[:, :], w[:, :], -1.0, 0.0, ALU.mult, ALU.max)
                chain.link(v.tensor_scalar(neg_f[:, :], w[:, :], 0.0, None, ALU.is_lt))
                v.scalar_tensor_tensor(k.sign_idx[:, 0:ET], src_f[:, :], 2.0, neg_f[:, :], ALU.mult, ALU.add)
                dve.wait_ge(made, 3)
                v.tensor_copy(k.iota[:, :], int_iota[:, :])
                v.tensor_copy(k.tile_base[:, :], int_base[:, :])
                dve.wait_ge(turned, 1)
                v.tensor_reduce(fold[:, :], ps_ends, AX.X, ALU.max).then_inc(folded, 1)
                dve.wait_ge(turned, 2)
                chain.link(v.tensor_copy(row[:, :], ps_row))
                chain.link(v.tensor_scalar(counts[:, 0:NG], row[:, NG:], -1.0, None, ALU.mult))
                chain.link(v.scalar_tensor_tensor(counts[:, NG:2 * NG], row[:, 0:NG], 1.0, row[:, NG:],
                                                  ALU.add, ALU.add))
                chain.link(v.tensor_tensor_scan(counts[:, 2 * NG:], ones[:, :], counts[:, NG:2 * NG], 0.0,
                                                ALU.mult, ALU.add))
                chain.link(v.tensor_tensor(counts[:, 2 * NG:], counts[:, 2 * NG:], counts[:, NG:2 * NG],
                                           ALU.subtract))
                chain.link(v.tensor_copy(k.bounds[:, :], counts[:, :]))

            @block.tensor
            def _(pe):
                pe.wait_ge(made, 3)
                pe.wait_ge(dve_step, 4)
                nc.tensor.transpose(ps_ends, ends[:, :], k.ident[:, :]).then_inc(turned, 1)
                pe.wait_ge(folded, 1)
                nc.tensor.transpose(ps_row, fold[:, :], k.ident[0:2 * NG, 0:2 * NG]).then_inc(turned, 1)


def gather_rows(k, pool, table, idx, width, sems):
    nc = k.nc
    for g in range(AHEAD):
        nc.gpsimd.tensor_copy(k.stage_idx[:, g, :], idx[:, g * G:(g + 1) * G]).then_inc(sems.staged, 1)
    with pool.Fori(0, NG // SLOTS) as i:
        for p in range(SLOTS):
            ahead = (p + AHEAD) % SLOTS
            pool.wait_ge(sems.seen, i * SLOTS + p + 1)
            pool.sem_inc(sems.fence, 1)
            nc.gpsimd.tensor_copy(k.stage_idx[:, ahead, :], idx[:, bass.ds((i * SLOTS + p + AHEAD) * G, G)])\
                .then_inc(sems.staged, 1)
            pool.wait_ge(sems.staged, i * SLOTS + p + 1)
            pool.wait_ge(sems.slot_free[p], i + 1)
            pool.sem_inc(sems.fence, 1)
            for t in range(G):
                pool.indirect_dma_start(k.rows[:, p, t, 0:width], None, table,
                                        bass.IndirectOffsetOnAxis(k.stage_idx[:, p, t:t + 1], 0))\
                    .then_inc(sems.rows[p], 16)
    for p in range(SLOTS):
        pool.wait_ge(sems.rows[p], GATHERED * (NG // SLOTS))


class PassSems:

    def __init__(self, sem):
        self.rows = [sem(f"rows{p}") for p in range(SLOTS)]
        self.slot_free = [sem(f"slot_free{p}") for p in range(SLOTS)]
        self.seen = sem("seen")
        self.staged = sem("staged")
        self.fence = sem("fence")
        self.dve_step = sem("dve_step")
        self.hot_ready = sem("hot_ready")
        self.sum_ready = sem("sum_ready")
        self.sum_free = sem("sum_free")


def window_tile(k, first, w):
    return k.nc.s_assert_within(first + w, 0, NT - 1,
                                skip_runtime_bounds_check_because="w counts the tiles up to the group's last")


def window_targets(k, dve, sems, g, tile, step):
    k.nc.vector.tensor_scalar(k.dst_rel[:, :], k.dst_f[:, bass.ds(g * G, G)],
                              k.tile_base[:, bass.ds(tile, 1)], None, ALU.subtract).then_inc(sems.dve_step, 1)
    dve.wait_ge(sems.dve_step, step)


def scatter_pass(k, tag, table, idx, width, cols, messages):
    nc, d = k.nc, k.dram
    with ExitStack() as ctx, semaphores(nc, tag) as sem:
        sems = PassSems(sem)
        sb = lambda name, shape: ctx.enter_context(nc.sbuf_tensor(f"{tag}_{name}", shape, FP32))
        made, weights_made = sem("made"), sem("weights_made")
        attr_free, edge_sum, relu_in = sem("attr_free"), sem("edge_sum"), sem("relu_in")
        attr_in = [sem(f"attr{p}") for p in range(SLOTS)]
        total = k.psum[:, 0, 0:cols]
        if messages == "edge":
            attr = sb("attr", [D, SLOTS, G * P])
            ps_edge = k.psum_cols(1, P, G * P).rearrange("p (t c) -> p t c", c=P)

        with nc.Block() as block:
            @block.gpsimd
            def _(pool):
                gather_rows(k, pool, table, idx, width, sems)

            @block.sync
            def _(sp):
                if messages != "edge":
                    return
                with sp.Fori(0, NG // SLOTS) as i:
                    for p in range(SLOTS):
                        sp.wait_ge(attr_free, i * SLOTS + p + 1)
                        sp.dma_start(attr[:, p, :], d["edge_attr_64"][:, bass.ds((i * SLOTS + p) * (G * P), G * P)])\
                            .then_inc(attr_in[p], 16)

            @block.vector
            def _(dve):
                v = nc.vector
                v.memset(k.acc[:, :, :], 0.0).then_inc(sems.dve_step, 1)
                dve.sem_inc(sems.seen, AHEAD)
                dve.sem_inc(sems.sum_free, 1)
                for p in range(SLOTS):
                    dve.sem_inc(sems.slot_free[p], 1)
                if messages == "edge":
                    v.memset(k.edge_a[:, :, H:H + 1], 1.0)
                with dve.Fori(0, NG // SLOTS) as i:
                    for p in range(SLOTS):
                        g = i * SLOTS + p
                        tile, count, before = group_bounds(dve, k, g)
                        dve.wait_ge(sems.rows[p], (i + 1) * GATHERED)
                        dve.sem_inc(sems.seen, 1)
                        by_edge = lambda a, c: a[:, bass.ds(g * G, G)].unsqueeze(2).broadcast_to([P, G, c])
                        if messages == "signed":
                            v.tensor_tensor(k.edge_a[:, :, 0:D], k.rows[:, p, :, 0:D], by_edge(k.wpos, D), ALU.mult)
                            v.tensor_tensor(k.edge_a[:, :, D:2 * D], k.rows[:, p, :, 0:D], by_edge(k.wneg, D),
                                            ALU.mult).then_inc(made, 1)
                        if messages == "edge":
                            for c, (a, b) in enumerate(CHUNKS):
                                dve.wait_ge(edge_sum, g * NC + c + 1)
                                v.tensor_tensor(k.edge_b[:, a:b, :], ps_edge[:, a:b, :], k.rows[:, p, a:b, :],
                                                ALU.add).then_inc(relu_in, 1)
                            v.tensor_copy(k.edge_a[:, :, H + 1:H + 2], by_edge(k.wpos, 1))
                            v.tensor_copy(k.edge_a[:, :, H + 2:H + 3], by_edge(k.wneg, 1)).then_inc(weights_made, 1)
                        with dve.Fori(0, count) as w:
                            at = window_tile(k, tile, w)
                            window_targets(k, dve, sems, g, at, (before + w) * 2 + 2)
                            for a, b in CHUNKS:
                                for t in range(a, b):
                                    last = v.tensor_scalar(k.hot[:, t, :], k.iota[:, :], k.dst_rel[:, t:t + 1], None,
                                                           ALU.is_equal)
                                last.then_inc(sems.hot_ready, 1)
                            dve.wait_ge(sems.sum_ready, before + w + 1)
                            v.tensor_tensor(k.acc[:, bass.ds(at, 1), 0:cols].rearrange("p a c -> p (a c)"),
                                            k.acc[:, bass.ds(at, 1), 0:cols].rearrange("p a c -> p (a c)"),
                                            total, ALU.add).then_inc(sems.dve_step, 1)
                            dve.wait_ge(sems.dve_step, (before + w) * 2 + 3)
                            dve.sem_inc(sems.sum_free, 1)
                        dve.sem_inc(sems.slot_free[p], 1)

            @block.scalar
            def _(act):
                if messages != "edge":
                    return
                with act.Fori(0, NG // SLOTS) as i:
                    for p in range(SLOTS):
                        g = i * SLOTS + p
                        for c, (a, b) in enumerate(CHUNKS):
                            act.wait_ge(relu_in, g * NC + c + 1)
                            last = nc.scalar.activation(k.edge_a[:, a:b, 0:H], k.edge_b[:, a:b, :], ACT.Relu)
                            last.then_inc(made, 1)

            @block.tensor
            def _(pe):
                if messages == "edge":
                    pe.sem_inc(attr_free, SLOTS)
                with pe.Fori(0, NG // SLOTS) as i:
                    for p in range(SLOTS):
                        g = i * SLOTS + p
                        _, count, before = group_bounds(pe, k, g)
                        if messages == "edge":
                            pe.wait_ge(attr_in[p], (i + 1) * 16)
                            for a, b in CHUNKS:
                                for t in range(a, b):
                                    last = nc.tensor.matmul(ps_edge[:, t, :], attr[:, p, t * P:(t + 1) * P],
                                                            k.weight["W1a_edge"][:, :], start=True, stop=True)
                                last.then_inc(edge_sum, 1)
                        if messages == "rows":
                            pe.wait_ge(sems.rows[p], (i + 1) * GATHERED)
                        elif messages == "signed":
                            pe.wait_ge(made, g + 1)
                        else:
                            pe.wait_ge(made, (g + 1) * NC)
                            pe.wait_ge(weights_made, g + 1)
                            pe.sem_inc(attr_free, 1)
                        pe.sem_inc(sems.fence, 1)
                        with pe.Fori(0, count) as w:
                            pe.wait_ge(sems.sum_free, before + w + 1)
                            for c, (a, b) in enumerate(CHUNKS):
                                pe.wait_ge(sems.hot_ready, (before + w) * NC + c + 1)
                                for t in range(a, b):
                                    rhs = k.rows[:, p, t, 0:width] if messages == "rows" else k.edge_a[:, t, 0:cols]
                                    last = nc.tensor.matmul(total, k.hot[:, t, :], rhs,
                                                            start=(t == 0), stop=(t == G - 1))
                            last.then_inc(sems.sum_ready, 1)


def gat_pass(k, tag, table):
    nc = k.nc
    with ExitStack() as ctx, semaphores(nc, tag) as sem:
        sems = PassSems(sem)
        sb = lambda name, shape: ctx.enter_context(nc.sbuf_tensor(f"{tag}_{name}", shape, FP32))
        turned, masked, turned_back, copied = sem("turned"), sem("masked"), sem("turned_back"), sem("copied")
        summed, leaky, max_ready, exp_ready, rescale_ready = sem("summed"), sem("leaky"), sem("max_ready"), sem("exp_ready"), sem("rescale")
        s_max, e_top, e_max, e_neg, e_old, rescale, d_now = (sb(n, [P, 1]) for n in
            ("s_max", "e_top", "e_max", "e_neg", "e_old", "rescale", "d_now"))
        s_part, scanned = sb("s_part", [P, NC]), sem("scanned")
        scores = k.edge_b[:, :, :]
        probs = k.big[:, 0:G, :]
        probs_by_edge = k.edge_a[:, :, 0:P]
        ps_s = k.psum_cols(0, P, G * P).rearrange("p (t c) -> p t c", c=P)
        ps_back = [k.psum_cols(4 + j, P, CH * P).rearrange("p (t c) -> p t c", c=P) for j in range(2)]
        total = k.psum[:, 6, 0:D + 1]
        STEPS = 7

        with nc.Block() as block:
            @block.gpsimd
            def _(pool):
                gather_rows(k, pool, table, k.src_idx, ZROW, sems)

            @block.vector
            def _(dve):
                v = nc.vector
                v.memset(k.acc[:, :, :], 0.0).then_inc(sems.dve_step, 1)
                dve.sem_inc(sems.seen, AHEAD)
                dve.sem_inc(sems.sum_free, 1)
                for p in range(SLOTS):
                    dve.sem_inc(sems.slot_free[p], 1)
                with dve.Fori(0, NG // SLOTS) as i:
                    for p in range(SLOTS):
                        g = i * SLOTS + p
                        first, count, before = group_bounds(dve, k, g)
                        dve.wait_ge(sems.rows[p], (i + 1) * GATHERED)
                        dve.sem_inc(sems.seen, 1)
                        with dve.Fori(0, count) as w:
                            at, n = window_tile(k, first, w), before + w
                            column = lambda a: a[:, bass.ds(at, 1)]
                            v.tensor_copy(d_now[:, :], column(k.d_low))
                            v.tensor_copy(e_old[:, :], column(k.e_best))
                            window_targets(k, dve, sems, g, at, n * STEPS + 2)
                            for a, b in CHUNKS:
                                for t in range(a, b):
                                    last = v.tensor_scalar(k.hot[:, t, :], k.iota[:, :], k.dst_rel[:, t:t + 1],
                                                           k.rows[:, p, t, D + 1:D + 2], ALU.is_equal, ALU.mult)
                                last.then_inc(sems.hot_ready, 1)
                            for c, (a, b) in enumerate(CHUNKS):
                                dve.wait_ge(turned, n * NC + c + 1)
                                v.tensor_reduce(s_part[:, c:c + 1], ps_s[:, a:b, :].rearrange("p t c -> p (t c)"),
                                                AX.X, ALU.max).then_inc(scanned, 1)
                            dve.wait_ge(scanned, (n + 1) * NC)
                            v.tensor_reduce(s_max[:, :], s_part[:, :], AX.X, ALU.max).then_inc(sems.dve_step, 1)
                            dve.wait_ge(sems.dve_step, n * STEPS + 3)
                            v.scalar_tensor_tensor(e_top[:, :], s_max[:, :], column(k.s_best), d_now[:, :],
                                                   ALU.max, ALU.add).then_inc(sems.dve_step, 1)
                            dve.wait_ge(sems.dve_step, n * STEPS + 4)
                            v.tensor_tensor(column(k.s_best), column(k.s_best), s_max[:, :], ALU.max)\
                                .then_inc(sems.dve_step, 1)
                            v.scalar_tensor_tensor(e_max[:, :], e_top[:, :], SLOPE, e_top[:, :], ALU.mult,
                                                   ALU.max).then_inc(sems.dve_step, 1)
                            dve.wait_ge(sems.dve_step, n * STEPS + 6)
                            v.tensor_scalar(e_neg[:, :], e_max[:, :], -1.0, None, ALU.mult).then_inc(max_ready, 1)
                            v.tensor_copy(column(k.e_best), e_max[:, :]).then_inc(sems.dve_step, 1)
                            for c, (a, b) in enumerate(CHUNKS):
                                dve.wait_ge(summed, n * NC + c + 1)
                                part = scores[:, a:b, :].rearrange("p t c -> p (t c)")
                                v.scalar_tensor_tensor(part, part, SLOPE, part, ALU.mult, ALU.max).then_inc(leaky, 1)
                            for c, (a, b) in enumerate(CHUNKS):
                                dve.wait_ge(exp_ready, n * NC + c + 1)
                                v.scalar_tensor_tensor(probs[:, a:b, :].rearrange("p t c -> p (t c)"),
                                                       ps_s[:, a:b, :].rearrange("p t c -> p (t c)"), 0.0,
                                                       scores[:, a:b, :].rearrange("p t c -> p (t c)"),
                                                       ALU.is_gt, ALU.mult).then_inc(masked, 1)
                            dve.wait_ge(rescale_ready, n + 1)
                            dve.wait_ge(sems.sum_ready, n + 1)
                            here = k.acc[:, bass.ds(at, 1), 0:D + 1].rearrange("p a c -> p (a c)")
                            v.scalar_tensor_tensor(here, here, rescale[:, :], total, ALU.mult, ALU.add)\
                                .then_inc(sems.dve_step, 1)
                            dve.wait_ge(sems.dve_step, n * STEPS + 8)
                            dve.sem_inc(sems.sum_free, 1)
                        dve.sem_inc(sems.slot_free[p], 1)

            @block.scalar
            def _(act):
                with act.Fori(0, NG // SLOTS) as i:
                    for p in range(SLOTS):
                        _, count, before = group_bounds(act, k, i * SLOTS + p)
                        with act.Fori(0, count) as w:
                            n = before + w
                            for c, (a, b) in enumerate(CHUNKS):
                                act.wait_ge(scanned, n * NC + c + 1)
                                nc.scalar.activation(scores[:, a:b, :], ps_s[:, a:b, :], ACT.Identity,
                                                     bias=d_now[:, :]).then_inc(summed, 1)
                            act.wait_ge(max_ready, n + 1)
                            for c, (a, b) in enumerate(CHUNKS):
                                act.wait_ge(leaky, n * NC + c + 1)
                                nc.scalar.activation(scores[:, a:b, :], scores[:, a:b, :], ACT.Exp,
                                                     bias=e_neg[:, :]).then_inc(exp_ready, 1)
                            nc.scalar.activation(rescale[:, :], e_old[:, :], ACT.Exp, bias=e_neg[:, :])\
                                .then_inc(rescale_ready, 1)
                            for c, (a, b) in enumerate(CHUNKS):
                                act.wait_ge(turned_back, n * NC + c + 1)
                                nc.scalar.copy(probs_by_edge[:, a:b, :], ps_back[c % 2][:, 0:b - a, :])\
                                    .then_inc(copied, 1)

            @block.tensor
            def _(pe):
                t_ = nc.tensor
                with pe.Fori(0, NG // SLOTS) as i:
                    for p in range(SLOTS):
                        _, count, before = group_bounds(pe, k, i * SLOTS + p)
                        with pe.Fori(0, count) as w:
                            n = before + w

                            def turn_back(c):
                                a, b = CHUNKS[c]
                                pe.wait_ge(masked, n * NC + c + 1)
                                if c >= 2:
                                    pe.wait_ge(copied, n * NC + c - 1)
                                for t in range(a, b):
                                    last = t_.transpose(ps_back[c % 2][:, t - a, :], probs[:, t, :], k.ident[:, :])
                                last.then_inc(turned_back, 1)

                            def sum_up(c):
                                a, b = CHUNKS[c]
                                pe.wait_ge(copied, n * NC + c + 1)
                                for t in range(a, b):
                                    last = t_.matmul(total, probs_by_edge[:, t, :], k.rows[:, p, t, 0:D + 1],
                                                     start=(t == 0), stop=(t == G - 1))
                                return last

                            pe.wait_ge(sems.sum_free, n + 1)
                            for c, (a, b) in enumerate(CHUNKS):
                                pe.wait_ge(sems.hot_ready, n * NC + c + 1)
                                for t in range(a, b):
                                    last = t_.transpose(ps_s[:, t, :], k.hot[:, t, :], k.ident[:, :])
                                last.then_inc(turned, 1)
                            turn_back(0)
                            for c in range(1, NC):
                                turn_back(c)
                                sum_up(c - 1)
                            sum_up(NC - 1).then_inc(sems.sum_ready, 1)


def over_columns(a, count):
    return a.unsqueeze(2).broadcast_to([a.shape[0], a.shape[1], count])


def over_tiles(a, tiles):
    return a.unsqueeze(1).broadcast_to([a.shape[0], tiles, a.shape[1]])


class NodePhase:

    def __init__(self, k, tag):
        self.k, self.tag = k, tag
        self.before = self.load = self.store = self.after = None
        self.w_mid = self.w_out = self.mid_bias = None
        self.kdim = self.cols = 0
        self.roots_before = self.roots_after = 0
        self.tables = []
        self.step_table = None
        self.least = False
        self.global_bias = False

    def build(self):
        k, nc, tag = self.k, self.k.nc, self.tag
        with semaphores(nc, tag) as sem:
            fence = sem("fence")
            step, staged, turned, copied = sem("step"), sem("staged"), sem("turned"), sem("copied")
            mid_sum, mid_ready, out_sum, table_free = sem("mid_sum"), sem("mid_ready"), sem("out_sum"), sem("table_free")
            self.inner = sem("inner")
            self.root_in, self.root_out = sem("root_in"), sem("root_out")
            self.fold_in, self.fold_out = sem("fold_in"), sem("fold_out")
            table_ready, written, stored, ready = sem("table_ready"), sem("written"), sem("stored"), sem("ready")
            ps_t = k.psum_cols(0, max(self.kdim, 1), NB * P)
            ps_mid = k.psum_cols(2, H, NB * P)
            width = P if self.cols <= P else 512
            ps_out = k.psum_cols(3 if width > P else 4, P, NB * width).rearrange("p (t c) -> p t c", c=width)

            with nc.Block() as block:
                @block.vector
                def _(dve):
                    chain = Chain(dve, step)
                    if self.before:
                        self.before(dve, chain)
                    if self.load:
                        with dve.Fori(0, NSTEP) as i:
                            self.load(i).then_inc(staged, 1)
                            dve.wait_ge(out_sum, i + 1)
                            if self.step_table:
                                dve.wait_ge(table_free, i + 1)
                            self.store(i, ps_out[:, :, 0:self.cols]).then_inc(stored, 1)
                            dve.wait_ge(stored, i + 1)
                    if self.after:
                        self.after(dve, chain)
                    v_done = nc.vector.memset(k.per_node[:, 3, 0:1], 0.0)
                    v_done.then_inc(table_ready, 1)

                @block.tensor
                def _(pe):
                    if self.global_bias:
                        nc.tensor.matmul(k.psum[:, 7, 0:1], k.weight["W2a_u"][:, :], k.weight["c_u"][:, :],
                                         start=True, stop=True).then_inc(self.fold_out, 1)
                    if self.load:
                        with pe.Fori(0, NSTEP) as i:
                            pe.wait_ge(staged, i + 1)
                            pe.sem_inc(fence, 1)
                            for j in range(NB):
                                last = nc.tensor.transpose(ps_t[:, j * P:(j + 1) * P],
                                                           k.node_in[:, j, 0:self.kdim], k.ident[:, :])
                            last.then_inc(turned, 1)
                            pe.wait_ge(copied, i + 1)
                            pe.sem_inc(fence, 1)
                            turned_in = k.node_inT
                            if self.w_mid is not None:
                                for a, b in ((0, 512), (512, NB * P)):
                                    last = nc.tensor.matmul(ps_mid[:, a:b], self.w_mid, k.node_inT[0:self.kdim, a:b],
                                                            start=True, stop=True)
                                last.then_inc(mid_sum, 1)
                                pe.wait_ge(mid_ready, i + 1)
                                turned_in = k.node_midT
                            rows = self.w_out.shape[0]
                            for j in range(NB):
                                last = nc.tensor.matmul(ps_out[:, j, 0:self.cols], turned_in[0:rows, j * P:(j + 1) * P],
                                                        self.w_out, start=True, stop=True)
                            last.then_inc(out_sum, 1)
                    if self.least:
                        pe.wait_ge(self.fold_in, 1)
                        nc.tensor.transpose(k.psum[0:1, 7, 0:P], k.per_node[:, 0, 0:1], k.ident[:, :])\
                            .then_inc(self.fold_out, 1)
                        pe.wait_ge(self.fold_in, 2)
                        nc.tensor.matmul(k.psum[:, 7, 256:257], k.ones[0:1, :], k.per_node[0:1, 0, 1:2],
                                         start=True, stop=True).then_inc(self.fold_out, 1)

                @block.scalar
                def _(act):
                    roots = 0
                    for _ in range(self.roots_before):
                        roots += 1
                        act.wait_ge(self.root_in, roots)
                        nc.scalar.activation(k.std[:, :, :], k.var[:, :, :], ACT.Sqrt).then_inc(self.root_out, 1)
                    if self.load:
                        with act.Fori(0, NSTEP) as i:
                            act.wait_ge(turned, i + 1)
                            nc.scalar.copy(k.node_inT[0:self.kdim, :], ps_t[:, :]).then_inc(copied, 1)
                            if self.w_mid is not None:
                                act.wait_ge(mid_sum, i + 1)
                                nc.scalar.activation(k.node_midT[:, :], ps_mid[:, :], ACT.Relu, bias=self.mid_bias)\
                                    .then_inc(mid_ready, 1)
                    for _ in range(self.roots_after):
                        roots += 1
                        act.wait_ge(self.root_in, roots)
                        nc.scalar.activation(k.std[:, :, :], k.var[:, :, :], ACT.Sqrt).then_inc(self.root_out, 1)

                @block.sync
                def _(sp):
                    if self.step_table:
                        to, source = self.step_table
                        sp.sem_inc(table_free, 1)
                        with sp.Fori(0, NSTEP) as i:
                            sp.wait_ge(stored, i + 1)
                            sp.dma_start(to[:, bass.ds(i * NB, NB), :], source).then_inc(written, 16)
                            sp.wait_ge(written, (i + 1) * 16)
                            sp.sem_inc(table_free, 1)
                    if self.tables:
                        sp.wait_ge(table_ready, 1)
                        for to, source in self.tables:
                            sp.dma_start(to, source).then_inc(written, 16)
                        sp.wait_ge(written, 16 * len(self.tables))


def root(phase, dve):
    dve.sem_inc(phase.root_in, 1)


def layer_norm(phase, dve, chain, roots):
    k, v = phase.k, phase.k.nc.vector
    mean, spread = k.per_node[:, 0, :], k.per_node[:, 1, :]
    chain.link(v.tensor_reduce(mean, k.h[:, :, :], AX.X, ALU.add))
    chain.link(v.tensor_scalar(mean, mean, -1.0 / D, None, ALU.mult))
    chain.link(v.tensor_tensor(k.h[:, :, :], k.h[:, :, :], over_columns(mean, D), ALU.add))
    chain.link(v.tensor_tensor(k.big[:, :, 0:D], k.h[:, :, :], k.h[:, :, :], ALU.mult))
    chain.link(v.tensor_reduce(spread, k.big[:, :, 0:D], AX.X, ALU.add))
    v.memset(k.var[:, :, 1:2], 1.0)
    v.tensor_scalar(k.var[:, :, 0], spread, 1.0 / D, EPS, ALU.mult, ALU.add).then_inc(phase.root_in, 1)
    dve.wait_ge(phase.root_out, roots)
    chain.link(v.reciprocal(spread, k.std[:, :, 0]))
    chain.link(v.tensor_tensor(k.x[:, :, :], k.h[:, :, :], over_columns(spread, D), ALU.mult))


def gat_finish(k, chain, relu):
    v = k.nc.vector
    rest = k.per_node[:, 0, :]
    chain.link(v.tensor_scalar(rest, k.acc[:, :, D], 1e-30, None, ALU.max))
    chain.link(v.reciprocal(rest, rest))
    chain.link(v.tensor_tensor(k.h[:, :, :], k.acc[:, :, 0:D], over_columns(rest, D), ALU.mult))
    if relu:
        chain.link(v.tensor_scalar(k.h[:, :, :], k.h[:, :, :], 0.0, None, ALU.max))


def gat_table(k, layer, table):
    phase, v = NodePhase(k, f"gt{layer}"), k.nc.vector
    w = k.weight
    source = k.x if layer == 0 else k.h
    phase.kdim, phase.cols, phase.w_out = D, D, w[f"W0{layer}"][:, :]
    phase.least = True
    if layer:
        phase.before = lambda dve, chain: gat_finish(k, chain, True)
    phase.load = lambda i: v.tensor_copy(k.node_in[:, :, 0:D], source[:, bass.ds(i * NB, NB), :])
    phase.store = lambda i, ps: v.tensor_tensor(k.z[:, bass.ds(i * NB, NB), 0:D], ps,
                                                over_tiles(w[f"b_0{layer}"][:, :], NB), ALU.add)

    def after(dve, chain):
        s, d = k.per_node[:, 1, :], k.per_node[:, 2, :]
        z = k.z[:, :, 0:D]
        v.memset(k.z[:, :, D:D + 1], 1.0)
        chain.link(v.tensor_tensor(k.big[:, :, 0:D], z, over_tiles(w[f"a_src{layer}"][:, :], NT), ALU.mult))
        v.tensor_tensor(k.big[:, :, D:2 * D], z, over_tiles(w[f"a_dst{layer}"][:, :], NT), ALU.mult)
        chain.link(v.tensor_reduce(s, k.big[:, :, 0:D], AX.X, ALU.add))
        chain.link(v.tensor_reduce(d, k.big[:, :, D:2 * D], AX.X, ALU.add))
        v.tensor_reduce(k.per_node[:, 0, 0:1], s, AX.X, ALU.min).then_inc(phase.fold_in, 1)
        dve.wait_ge(phase.fold_out, 1)
        v.tensor_reduce(k.per_node[0:1, 0, 1:2], k.psum[0:1, 7, 0:P], AX.X, ALU.min).then_inc(phase.fold_in, 1)
        dve.wait_ge(phase.fold_out, 2)
        chain.link(v.tensor_scalar(k.per_node[:, 0, 2:3], k.psum[:, 7, 256:257], -1.0, None, ALU.add))
        low = k.per_node[:, 0, 2:3]
        v.tensor_scalar(k.z[:, :, D + 1], s, low, None, ALU.subtract)
        chain.link(v.tensor_scalar(k.d_low[:, :], d, w[f"b_att{layer}"][:, :], low, ALU.add, ALU.add))
        v.memset(k.s_best[:, :], 0.0)
        chain.link(v.scalar_tensor_tensor(k.e_best[:, :], k.d_low[:, :], SLOPE, k.d_low[:, :], ALU.mult, ALU.max))

    phase.after = after
    phase.tables = [(table.rearrange("(t p) f -> p t f", p=P), k.z[:, :, :])]
    phase.build()


def edge_table(k, table):
    phase, v = NodePhase(k, "et"), k.nc.vector
    phase.kdim, phase.cols, phase.w_out = D, H, k.weight["W1a_node"][:, :]
    phase.roots_before = 1

    def before(dve, chain):
        gat_finish(k, chain, False)
        chain.link(v.tensor_tensor(k.h[:, :, :], k.h[:, :, :], k.x[:, :, :], ALU.add))
        layer_norm(phase, dve, chain, 1)

    phase.before = before
    phase.load = lambda i: v.tensor_copy(k.node_in[:, :, 0:D], k.x[:, bass.ds(i * NB, NB), :])
    phase.store = lambda i, ps: v.tensor_tensor(k.table[:, bass.ds(i * NB, NB), :], ps,
                                                over_tiles(k.weight["b_1a"][:, :], NB), ALU.add)
    phase.tables = [(table.rearrange("(t p) f -> p t f", p=P), k.table[:, :, :])]
    phase.build()


def edge_mean(k):
    phase, v = NodePhase(k, "em"), k.nc.vector
    phase.kdim, phase.cols, phase.w_out = H, D, k.weight["W1b"][:, :]
    phase.roots_before = 1
    share, any_edge = k.per_node[:, 1, :], k.per_node[:, 2, :]

    def before(dve, chain):
        chain.link(v.tensor_scalar(share, k.acc[:, :, H], 1.0, None, ALU.max))
        chain.link(v.reciprocal(share, share))
        v.tensor_scalar(any_edge, k.acc[:, :, H], 1.0, None, ALU.min)
        v.tensor_copy(k.big[:, :, 0:D], k.x[:, :, :])
        chain.link(v.tensor_scalar(k.var[:, :, :], k.acc[:, :, H + 1:H + 3], 1.0, None, ALU.add))
        dve.sem_inc(phase.root_in, 1)
        dve.wait_ge(phase.root_out, 1)
        chain.link(v.reciprocal(k.dinv[:, :, :], k.std[:, :, :]))

    def store(i, ps):
        mean = k.big[:, bass.ds(i * NB, NB), D:2 * D]
        k.nc.vector.tensor_tensor(k.edge_b[:, 0:NB, 0:D], over_tiles(k.weight["b_1b"][:, :], NB),
                                  over_columns(k.per_node[:, 2, bass.ds(i * NB, NB)], D), ALU.mult)\
            .then_inc(phase.inner, 1)
        k.nc.vector.wait_ge(phase.inner, i + 1)
        return v.tensor_tensor(mean, ps, k.edge_b[:, 0:NB, 0:D], ALU.add)

    phase.before, phase.store = before, store
    phase.load = lambda i: v.tensor_tensor(k.node_in[:, :, :], k.acc[:, bass.ds(i * NB, NB), 0:H],
                                           over_columns(k.per_node[:, 1, bass.ds(i * NB, NB)], H), ALU.mult)
    phase.build()


def node_mlp(k):
    phase, v = NodePhase(k, "nm"), k.nc.vector
    phase.kdim, phase.cols = 2 * D, D
    phase.w_mid, phase.w_out = k.weight["W2a"][:, :], k.weight["W2b"][:, :]
    phase.mid_bias = k.per_node[:, 3, 1:2]
    phase.global_bias, phase.roots_after = True, 1

    def before(dve, chain):
        dve.wait_ge(phase.fold_out, 1)
        chain.link(v.tensor_tensor(k.per_node[:, 3, 1:2], k.psum[:, 7, 0:1], k.weight["c_2a"][:, :], ALU.add))

    def after(dve, chain):
        chain.link(v.tensor_tensor(k.h[:, :, :], k.h[:, :, :], over_tiles(k.weight["b_2b"][:, :], NT), ALU.add))
        layer_norm(phase, dve, chain, 1)

    phase.before, phase.after = before, after
    phase.load = lambda i: v.tensor_copy(k.node_in[:, :, :], k.big[:, bass.ds(i * NB, NB), :])
    phase.store = lambda i, ps: v.tensor_tensor(k.h[:, bass.ds(i * NB, NB), :], ps,
                                                k.x[:, bass.ds(i * NB, NB), :], ALU.add)
    phase.build()


def relation_table(k, table):
    phase, v = NodePhase(k, "rt"), k.nc.vector
    phase.kdim, phase.cols, phase.w_out = D, RELS * D, k.weight["Wrel"][:, :]
    phase.load = lambda i: v.tensor_copy(k.node_in[:, :, 0:D], k.x[:, bass.ds(i * NB, NB), :])
    phase.store = lambda i, ps: v.tensor_copy(k.wide_table[:, :, :], ps)
    phase.step_table = (table.rearrange("(t p r) f -> p t (r f)", p=P, r=RELS), k.wide_table[:, :, :])
    phase.build()


def signed_table(k, table):
    phase, v = NodePhase(k, "st"), k.nc.vector
    phase.kdim, phase.cols, phase.w_out = D, D, k.weight["Wself"][:, :]
    phase.roots_after = 1
    phase.load = lambda i: v.tensor_copy(k.node_in[:, :, 0:D], k.x[:, bass.ds(i * NB, NB), :])
    phase.store = lambda i, ps: v.tensor_tensor(k.h[:, bass.ds(i * NB, NB), :], ps,
                                                k.acc[:, bass.ds(i * NB, NB), 0:D], ALU.add)

    def after(dve, chain):
        chain.link(v.scalar_tensor_tensor(k.h[:, :, :], k.h[:, :, :], 0.0, k.x[:, :, :], ALU.max, ALU.add))
        layer_norm(phase, dve, chain, 1)
        for j in range(2):
            chain.link(v.tensor_tensor(k.table[:, :, j * D:(j + 1) * D], k.x[:, :, :],
                                       over_columns(k.dinv[:, :, j], D), ALU.mult))

    phase.after = after
    phase.tables = [(table.rearrange("(t p r) f -> p t (r f)", p=P, r=2), k.table[:, :, :])]
    phase.build()


def gcn_sum(k, chain):
    v = k.nc.vector
    chain.link(v.tensor_tensor(k.acc[:, :, 0:H], k.acc[:, :, 0:H], k.table[:, :, :], ALU.add))
    chain.link(v.tensor_tensor(k.acc[:, :, 0:D], k.acc[:, :, 0:D], over_columns(k.dinv[:, :, 0], D), ALU.mult))
    chain.link(v.tensor_scalar(k.per_node[:, 0, :], k.dinv[:, :, 1], -1.0, None, ALU.mult))
    chain.link(v.tensor_tensor(k.acc[:, :, D:H], k.acc[:, :, D:H], over_columns(k.per_node[:, 0, :], D), ALU.mult))


def gcn_mid(k, table):
    phase, v = NodePhase(k, "gm"), k.nc.vector
    phase.kdim, phase.cols = 2 * D, 2 * D
    phase.w_mid, phase.w_out = k.weight["W3a"][:, :], k.weight["W3b"][:, :]
    phase.mid_bias = k.per_node[:, 3, 1:2]

    def before(dve, chain):
        gcn_sum(k, chain)
        chain.link(v.tensor_tensor(k.per_node[:, 3, 1:2], k.weight["c_3p"][:, :], k.weight["c_3n"][:, :],
                                   ALU.subtract))

    def after(dve, chain):
        for j in range(2):
            part = k.table[:, :, j * D:(j + 1) * D]
            chain.link(v.tensor_tensor(part, part, over_columns(k.dinv[:, :, j], D), ALU.mult))

    phase.before, phase.after = before, after
    phase.load = lambda i: v.tensor_copy(k.node_in[:, :, :], k.acc[:, bass.ds(i * NB, NB), 0:H])
    phase.store = lambda i, ps: v.tensor_copy(k.table[:, bass.ds(i * NB, NB), :], ps)
    phase.tables = [(table.rearrange("(t p r) f -> p t (r f)", p=P, r=2), k.table[:, :, :])]
    phase.build()


def gcn_finish(k, out):
    phase, v = NodePhase(k, "gf"), k.nc.vector
    phase.roots_after = 1

    def after(dve, chain):
        gcn_sum(k, chain)
        chain.link(v.tensor_tensor(k.h[:, :, :], k.acc[:, :, 0:D], k.acc[:, :, D:H], ALU.add))
        bias = k.edge_b[:, 0, 0:D]
        chain.link(v.tensor_tensor(bias, k.weight["b_3p"][:, :], k.weight["b_3n"][:, :], ALU.subtract))
        chain.link(v.tensor_tensor(k.h[:, :, :], k.h[:, :, :], over_tiles(bias, NT), ALU.add))
        chain.link(v.scalar_tensor_tensor(k.h[:, :, :], k.h[:, :, :], 0.0, k.x[:, :, :], ALU.max, ALU.add))
        layer_norm(phase, dve, chain, 1)

    phase.after = after
    phase.tables = [(out.rearrange("(t p) f -> p t f", p=P), k.x[:, :, :])]
    phase.build()



INPUTS = {
    "x": [NPAD, D], "src": [P, ET], "dst": [P, ET], "edge_type_8": [P, ET], "edge_weight": [P, ET],
    "edge_attr_64": [D, EPAD],
}
for layer in range(3):
    INPUTS.update({f"L0_gnn_W{layer}": [D, D], f"L0_gnn_b{layer}": [D], f"L0_gnn_a{layer}": [2, D],
                   f"L0_gnn_ab{layer}": [1]})
INPUTS.update({
    "L1_gnn_u": [16, D], "L1_gnn_W1a": [2 * D, H], "L1_gnn_b1a": [H], "L1_gnn_W1b": [H, D], "L1_gnn_b1b": [D],
    "L1_gnn_W2a": [3 * D, H], "L1_gnn_b2a": [H], "L1_gnn_W2b": [H, D], "L1_gnn_b2b": [D],
    "L2_gnn_weight": [D, RELS * D], "L2_gnn_self_loop_w": [D, D],
    "L3_gnn_W1": [2 * D, H], "L3_gnn_b1p": [H], "L3_gnn_b1n": [H], "L3_gnn_W2": [H, 2 * D],
    "L3_gnn_b2p": [D], "L3_gnn_b2n": [D],
})
INTS = ("src", "dst", "edge_type_8")


def program(nc, dram, out):
    with ExitStack() as ctx:
        k = Program(nc, ctx, dram)
        scratch = lambda name, rows, cols: nc.dram_tensor(name, (rows, cols), FP32, kind="Internal").ap()
        z_table, y_table = scratch("z_table", NPAD, ZROW), scratch("y_table", NPAD, H)
        rel_table, sign_table = scratch("rel_table", NPAD * RELS, D), scratch("sign_table", NPAD * 2, D)
        setup(k)
        for layer in range(3):
            gat_table(k, layer, z_table)
            gat_pass(k, f"g{layer}", z_table)
        edge_table(k, y_table)
        scatter_pass(k, "ep", y_table, k.src_idx, H, HROW, "edge")
        edge_mean(k)
        node_mlp(k)
        relation_table(k, rel_table)
        scatter_pass(k, "rp", rel_table, k.rel_idx, D, D, "rows")
        signed_table(k, sign_table)
        scatter_pass(k, "sp", sign_table, k.sign_idx, D, H, "signed")
        gcn_mid(k, sign_table)
        scatter_pass(k, "sq", sign_table, k.sign_idx, D, H, "signed")
        gcn_finish(k, out)


def layout(inputs):
    import numpy as np

    def edges(a, pad=0):
        padded = np.full(EPAD, pad, a.dtype)
        padded[:E] = a
        return np.ascontiguousarray(padded.reshape(ET, P).T)

    a = {name: np.asarray(value) for name, value in inputs.items()}
    got = {}
    got["x"] = np.zeros((NPAD, D), a["x"].dtype)
    got["x"][:N] = a["x"]
    for name in ("src", "edge_type_8", "edge_weight"):
        got[name] = edges(a[name])
    got["dst"] = edges(a["dst"], NPAD - 1)
    got["edge_attr_64"] = np.zeros((D, EPAD), a["edge_attr_64"].dtype)
    got["edge_attr_64"][:, :E] = a["edge_attr_64"].T
    for l in range(3):
        got[f"L0_gnn_W{l}"] = np.ascontiguousarray(a[f"L0_gnn_W{l}"].T)
        got[f"L0_gnn_b{l}"] = a[f"L0_gnn_b{l}"]
        got[f"L0_gnn_a{l}"] = a[f"L0_gnn_a{l}"].reshape(2, D)
        got[f"L0_gnn_ab{l}"] = a[f"L0_gnn_ab{l}"]
    got["L2_gnn_weight"] = np.ascontiguousarray(a["L2_gnn_weight"].transpose(1, 0, 2).reshape(D, RELS * D))
    got["L2_gnn_self_loop_w"] = np.ascontiguousarray(a["L2_gnn_self_loop_w"].T)
    got["L3_gnn_W1"] = np.concatenate([a["L3_gnn_W1p"].T, a["L3_gnn_W1n"].T], axis=0)
    got["L3_gnn_W2"] = np.concatenate([a["L3_gnn_W2p"].T, a["L3_gnn_W2n"].T], axis=1)
    return {name: got.get(name, a.get(name)) for name in INPUTS}


def kernel(**inputs):
    import concourse.bacc as bacc
    from concourse.bass_utils import run_bass_kernel_spmd as run

    nc = bacc.Bacc("TRN2", target_bir_lowering=False, num_devices=1)
    arrays = {"in_" + name: a for name, a in layout(inputs).items()}
    dram = {name: nc.dram_tensor("in_" + name, tuple(shape), INT32 if name in INTS else FP32, kind="ExternalInput").ap()
            for name, shape in INPUTS.items()}
    out = nc.dram_tensor("out", (NPAD, D), FP32, kind="ExternalOutput").ap()
    program(nc, dram, out)
    return run(nc, [arrays], core_ids=[0]).results[0]["out"][:N]
```

```python
import concourse.bass as bass
from concourse import mybir
from contextlib import ExitStack, contextmanager

FP32 = mybir.dt.float32
FP16 = mybir.dt.float16
UINT8 = mybir.dt.uint8
INT32 = mybir.dt.int32
ALU = mybir.AluOpType
ACT = mybir.ActivationFunctionType
AX = mybir.AxisListType

P = 128
N = 3125
E = 100000
D = 64
H = 128
RELS = 8
NT = -(-N // P)
NPAD = NT * P
G = 14
SLOTS = 4
NG = -(-E // (P * G * SLOTS)) * SLOTS
ET = NG * G
EPAD = ET * P
AHEAD = 2
CH = 4
CHUNKS = [(c, min(c + CH, G)) for c in range(0, G, CH)]
NC = len(CHUNKS)
NB = 5
NSTEP = NT // NB
GATHERED = 16 * G
WIN = 25
NWIN = NPAD // WIN
QW = 5
NQ = NT // QW
QC = QW * P
PAD_TILES = 4
BUILD = 2
SLOPE = 0.01
EPS = 1e-5
ZROW = D + 2
HROW = H + 3


WEIGHTS = [(f"W0{l}", D, D) for l in range(3)] + [(f"b_0{l}", P, D) for l in range(3)]
WEIGHTS += [(f"a_src{l}", P, D) for l in range(3)] + [(f"a_dst{l}", P, D) for l in range(3)]
WEIGHTS += [(f"b_att{l}", P, 1) for l in range(3)]
WEIGHTS += [
    ("W1a_node", D, H), ("W1a_edge", D, H), ("b_1a", P, H), ("W1b", H, D), ("b_1b", P, D),
    ("W2a", 2 * D, H), ("W2a_u", D, H), ("c_u", D, 1), ("c_2a", H, 1), ("W2b", H, D), ("b_2b", P, D),
    ("Wrel", D, RELS * D), ("Wself", D, D),
    ("W3a", 2 * D, H), ("c_3p", H, 1), ("c_3n", H, 1), ("W3b", H, 2 * D), ("b_3p", P, D), ("b_3n", P, D),
]


def weight_sources(d):
    row = lambda a: a.partition_broadcast(P)
    column = lambda a: a.rearrange("(n o) -> n o", o=1)
    at = {}
    for l in range(3):
        at[f"W0{l}"] = d[f"L0_gnn_W{l}"]
        at[f"b_0{l}"] = row(d[f"L0_gnn_b{l}"])
        at[f"a_src{l}"] = row(d[f"L0_gnn_a{l}"][0, :])
        at[f"a_dst{l}"] = row(d[f"L0_gnn_a{l}"][1, :])
        at[f"b_att{l}"] = row(d[f"L0_gnn_ab{l}"])
    at.update({
        "W1a_node": d["L1_gnn_W1a"][0:D, :], "W1a_edge": d["L1_gnn_W1a"][D:2 * D, :], "b_1a": row(d["L1_gnn_b1a"]),
        "W1b": d["L1_gnn_W1b"], "b_1b": row(d["L1_gnn_b1b"]), "W2a": d["L1_gnn_W2a"][0:2 * D, :],
        "W2a_u": d["L1_gnn_W2a"][2 * D:3 * D, :], "c_u": column(d["L1_gnn_u"][0, :]),
        "c_2a": column(d["L1_gnn_b2a"]), "W2b": d["L1_gnn_W2b"], "b_2b": row(d["L1_gnn_b2b"]),
        "Wrel": d["L2_gnn_weight"], "Wself": d["L2_gnn_self_loop_w"],
        "W3a": d["L3_gnn_W1"], "c_3p": column(d["L3_gnn_b1p"]), "c_3n": column(d["L3_gnn_b1n"]),
        "W3b": d["L3_gnn_W2"], "b_3p": row(d["L3_gnn_b2p"]), "b_3n": row(d["L3_gnn_b2n"]),
    })
    return at


@contextmanager
def semaphores(nc, tag):
    held = []

    def sem(name):
        held.append(nc.alloc_semaphore(f"{tag}_{name}"))
        return held[-1]

    yield sem
    nc.clear_and_free_semaphores(held)
    nc.all_engine_barrier()


class Chain:

    def __init__(self, eng, sem):
        self.eng, self.sem, self.n = eng, sem, 0

    def link(self, ins):
        self.n += 1
        ins.then_inc(self.sem, 1)
        self.eng.wait_ge(self.sem, self.n)


class Program:
    def __init__(self, nc, ctx, dram):
        self.nc, self.ctx, self.dram = nc, ctx, dram
        sb = self.sb
        self.x = sb("x", [P, NT, D])
        self.h = sb("h", [P, NT, D])
        self.acc = sb("acc", [P, NT, HROW])
        self.ident = sb("ident", [P, P])
        self.iota = sb("iota", [P, P])
        self.tile_base = sb("tile_base", [P, NT])
        self.src_idx = sb("src_idx", [P, ET + AHEAD * G], INT32)
        self.rel_idx = sb("rel_idx", [P, ET + AHEAD * G], INT32)
        self.sign_idx = sb("sign_idx", [P, ET + AHEAD * G], INT32)
        self.dst_f = sb("dst_f", [P, ET])
        self.wpos = sb("wpos", [P, ET])
        self.wneg = sb("wneg", [P, ET])
        self.bounds = sb("bounds", [1, 3 * NG], INT32)
        self.dinv = sb("dinv", [P, NT, 2])
        self.d_low = sb("d_low", [P, NT])
        self.per_node = sb("per_node", [P, 4, NT])
        self.var = sb("var", [P, NT, 2])
        self.std = sb("std", [P, NT, 2])
        self.ones = sb("ones", [P, P])
        self.z = sb("z", [P, NT, ZROW])
        self.table = sb("table", [P, NT, H])
        self.node_in = sb("node_in", [P, NB, H])
        self.node_inT = sb("node_inT", [P, NB * P])
        self.node_midT = sb("node_midT", [P, NB * P])
        self.node_out = sb("node_out", [P, NB, D])
        self.big = sb("big", [P, NT, H])
        self.s_turned = sb("s_turned", [NT, P])
        self.weight = {}
        for name, rows, cols in WEIGHTS:
            self.weight[name] = sb("w_" + name, [rows, cols])
        self.psum = ctx.enter_context(nc.psum_tensor("psum", [P, 8, 512], FP32))

    def sb(self, name, shape, dtype=FP32):
        return self.ctx.enter_context(self.nc.sbuf_tensor(name, shape, dtype))

    def psum_cols(self, first_bank, parts, cols):
        flat = self.psum[:, :, :].rearrange("p b c -> p (b c)")
        return flat[0:parts, 512 * first_bank:512 * first_bank + cols]


def group_bounds(eng, k, g):
    first = eng.value_load(k.bounds[0:1, bass.ds(g, 1)], min_val=0, max_val=NT - 1)
    count = eng.value_load(k.bounds[0:1, bass.ds(g + NG, 1)], min_val=1, max_val=NT)
    before = eng.value_load(k.bounds[0:1, bass.ds(g + 2 * NG, 1)], min_val=0, max_val=NT * NG)
    return first, count, before


def setup(k):
    nc, d = k.nc, k.dram
    with ExitStack() as ctx, semaphores(nc, "su") as sem:
        sb = lambda name, shape, dt=FP32: ctx.enter_context(nc.sbuf_tensor(name, shape, dt))
        weights = sem("weights")
        loaded, made, folded = sem("loaded"), sem("made"), sem("folded")
        turned, pool_step, dve_step = sem("turned"), sem("pool"), sem("dve")
        dst_i, type_i, w = sb("su_dst", [P, ET], INT32), sb("su_type", [P, ET], INT32), sb("su_w", [P, ET])
        tile_i, tile_f = sb("su_tile_i", [P, ET], INT32), sb("su_tile_f", [P, ET])
        ends, fold, row = sb("su_ends", [P, 2 * NG]), sb("su_fold", [2 * NG, 1]), sb("su_row", [1, 2 * NG])
        ones, counts = sb("su_ones", [1, NG]), sb("su_counts", [1, 3 * NG])
        neg_f = sb("su_neg_f", [P, ET])
        src_f, t_f = sb("su_src_f", [P, ET]), sb("su_t_f", [P, ET])
        int_iota, int_base = sb("su_iota", [P, P], INT32), sb("su_base", [P, NT], INT32)
        ps_ends = k.psum_cols(0, 2 * NG, P)
        ps_row = k.psum_cols(1, 1, 2 * NG)

        with nc.Block() as block:
            @block.sync
            def _(sp):
                sp.dma_start(k.x[:, :, :], d["x"].rearrange("(t p) f -> p t f", p=P)).then_inc(loaded, 16)
                sp.dma_start(k.src_idx[:, 0:ET], d["src"]).then_inc(loaded, 16)
                sp.dma_start(dst_i[:, :], d["dst"]).then_inc(loaded, 16)
                sp.dma_start(type_i[:, :], d["edge_type_8"]).then_inc(loaded, 16)
                sp.dma_start(w[:, :], d["edge_weight"]).then_inc(loaded, 16)
                for name, source in weight_sources(d).items():
                    sp.dma_start(k.weight[name][:, :], source).then_inc(weights, 16)
                sp.wait_ge(weights, 16 * len(WEIGHTS))

            @block.gpsimd
            def _(pool):
                nc.gpsimd.memset(k.ident[:, :], 0.0).then_inc(pool_step, 1)
                nc.gpsimd.iota(int_iota[:, :], pattern=[[1, P]], base=0, channel_multiplier=0).then_inc(made, 1)
                nc.gpsimd.iota(int_base[:, :], pattern=[[P, NT]], base=0, channel_multiplier=0).then_inc(made, 1)
                for idx in (k.src_idx, k.rel_idx, k.sign_idx):
                    nc.gpsimd.memset(idx[:, ET:], 0)
                pool.wait_ge(pool_step, 1)
                nc.gpsimd.affine_select(out=k.ident[:, :], in_=k.ident[:, :], compare_op=ALU.not_equal,
                                        fill=1.0, base=0, pattern=[[-1, P]], channel_multiplier=1).then_inc(made, 1)

            @block.vector
            def _(dve):
                v, chain = nc.vector, Chain(dve, dve_step)
                v.memset(ones[:, :], 1.0)
                v.memset(k.ones[:, :], 1.0)
                dve.wait_ge(loaded, 5 * 16)
                chain.link(v.tensor_scalar(tile_i[:, :], dst_i[:, :], 7, None, ALU.arith_shift_right))
                chain.link(v.tensor_copy(tile_f[:, :], tile_i[:, :]))
                per_group = tile_f[:, :].rearrange("p (g t) -> p g t", t=G)
                v.tensor_reduce(ends[:, 0:NG], per_group, AX.X, ALU.max)
                chain.link(v.tensor_reduce(ends[:, NG:], per_group, AX.X, ALU.min))
                chain.link(v.tensor_scalar(ends[:, NG:], ends[:, NG:], -1.0, None, ALU.mult))
                v.tensor_copy(k.dst_f[:, :], dst_i[:, :])
                v.tensor_copy(src_f[:, :], k.src_idx[:, 0:ET])
                chain.link(v.tensor_copy(t_f[:, :], type_i[:, :]))
                v.scalar_tensor_tensor(k.rel_idx[:, 0:ET], src_f[:, :], float(RELS), t_f[:, :], ALU.mult, ALU.add)
                v.tensor_scalar(k.wpos[:, :], w[:, :], 0.0, None, ALU.max)
                v.tensor_scalar(k.wneg[:, :], w[:, :], -1.0, 0.0, ALU.mult, ALU.max)
                chain.link(v.tensor_scalar(neg_f[:, :], w[:, :], 0.0, None, ALU.is_lt))
                v.scalar_tensor_tensor(k.sign_idx[:, 0:ET], src_f[:, :], 2.0, neg_f[:, :], ALU.mult, ALU.add)
                dve.wait_ge(made, 3)
                v.tensor_copy(k.iota[:, :], int_iota[:, :])
                v.tensor_copy(k.tile_base[:, :], int_base[:, :])
                dve.wait_ge(turned, 1)
                v.tensor_reduce(fold[:, :], ps_ends, AX.X, ALU.max).then_inc(folded, 1)
                dve.wait_ge(turned, 2)
                chain.link(v.tensor_copy(row[:, :], ps_row))
                chain.link(v.tensor_scalar(counts[:, 0:NG], row[:, NG:], -1.0, None, ALU.mult))
                chain.link(v.scalar_tensor_tensor(counts[:, NG:2 * NG], row[:, 0:NG], 1.0, row[:, NG:],
                                                  ALU.add, ALU.add))
                chain.link(v.tensor_tensor_scan(counts[:, 2 * NG:], ones[:, :], counts[:, NG:2 * NG], 0.0,
                                                ALU.mult, ALU.add))
                chain.link(v.tensor_tensor(counts[:, 2 * NG:], counts[:, 2 * NG:], counts[:, NG:2 * NG],
                                           ALU.subtract))
                chain.link(v.tensor_copy(k.bounds[:, :], counts[:, :]))

            @block.tensor
            def _(pe):
                pe.wait_ge(made, 3)
                pe.wait_ge(dve_step, 4)
                nc.tensor.transpose(ps_ends, ends[:, :], k.ident[:, :]).then_inc(turned, 1)
                pe.wait_ge(folded, 1)
                nc.tensor.transpose(ps_row, fold[:, :], k.ident[0:2 * NG, 0:2 * NG]).then_inc(turned, 1)


def gather_rows(k, buf, pool, table, idx, width, sems):
    nc = k.nc
    for g in range(AHEAD):
        nc.gpsimd.tensor_copy(buf.stage_idx[:, g, :], idx[:, g * G:(g + 1) * G]).then_inc(sems.staged, 1)
    with pool.Fori(0, NG // SLOTS) as i:
        for p in range(SLOTS):
            ahead = (p + AHEAD) % SLOTS
            pool.wait_ge(sems.seen, i * SLOTS + p + 1)
            pool.sem_inc(sems.fence, 1)
            nc.gpsimd.tensor_copy(buf.stage_idx[:, ahead, :], idx[:, bass.ds((i * SLOTS + p + AHEAD) * G, G)])\
                .then_inc(sems.staged, 1)
            pool.wait_ge(sems.staged, i * SLOTS + p + 1)
            pool.wait_ge(sems.slot_free[p], i + 1)
            pool.sem_inc(sems.fence, 1)
            for t in range(G):
                pool.indirect_dma_start(buf.rows[:, p, t, 0:width], None, table,
                                        bass.IndirectOffsetOnAxis(buf.stage_idx[:, p, t:t + 1], 0))\
                    .then_inc(sems.rows[p], 16)
    for p in range(SLOTS):
        pool.wait_ge(sems.rows[p], GATHERED * (NG // SLOTS))


class PassBuffers:

    def __init__(self, sb):
        self.rows = sb("rows", [P, SLOTS, G, H])
        self.stage_idx = sb("stage_idx", [P, SLOTS, G], INT32)
        self.hot = sb("hot", [P, G, P])
        self.edge_a = sb("edge_a", [P, G, HROW])
        self.edge_b = sb("edge_b", [P, G, P])
        self.dst_rel = sb("dst_rel", [P, G])


class PassSems:

    def __init__(self, sem):
        self.rows = [sem(f"rows{p}") for p in range(SLOTS)]
        self.slot_free = [sem(f"slot_free{p}") for p in range(SLOTS)]
        self.seen = sem("seen")
        self.staged = sem("staged")
        self.fence = sem("fence")
        self.dve_step = sem("dve_step")
        self.hot_ready = sem("hot_ready")
        self.sum_ready = sem("sum_ready")
        self.sum_free = sem("sum_free")


def window_tile(k, first, w):
    return k.nc.s_assert_within(first + w, 0, NT - 1,
                                skip_runtime_bounds_check_because="w counts the tiles up to the group's last")


def window_targets(k, buf, dve, sems, g, tile, step):
    k.nc.vector.tensor_scalar(buf.dst_rel[:, :], k.dst_f[:, bass.ds(g * G, G)],
                              k.tile_base[:, bass.ds(tile, 1)], None, ALU.subtract).then_inc(sems.dve_step, 1)
    dve.wait_ge(sems.dve_step, step)


def scatter_pass(k, tag, table, idx, width, cols, messages):
    nc, d = k.nc, k.dram
    with ExitStack() as ctx, semaphores(nc, tag) as sem:
        sems = PassSems(sem)
        sb = lambda name, shape, dt=FP32: ctx.enter_context(nc.sbuf_tensor(f"{tag}_{name}", shape, dt))
        buf = PassBuffers(sb)
        made, weights_made = sem("made"), sem("weights_made")
        attr_free, edge_sum, relu_in = sem("attr_free"), sem("edge_sum"), sem("relu_in")
        attr_in = [sem(f"attr{p}") for p in range(SLOTS)]
        total = k.psum[:, 0, 0:cols]
        if messages == "edge":
            attr = sb("attr", [D, SLOTS, G * P])
            ps_edge = k.psum_cols(1, P, G * P).rearrange("p (t c) -> p t c", c=P)

        with nc.Block() as block:
            @block.gpsimd
            def _(pool):
                gather_rows(k, buf, pool, table, idx, width, sems)

            @block.sync
            def _(sp):
                if messages != "edge":
                    return
                with sp.Fori(0, NG // SLOTS) as i:
                    for p in range(SLOTS):
                        sp.wait_ge(attr_free, i * SLOTS + p + 1)
                        sp.dma_start(attr[:, p, :], d["edge_attr_64"][:, bass.ds((i * SLOTS + p) * (G * P), G * P)])\
                            .then_inc(attr_in[p], 16)

            @block.vector
            def _(dve):
                v = nc.vector
                v.memset(k.acc[:, :, :], 0.0).then_inc(sems.dve_step, 1)
                dve.sem_inc(sems.seen, AHEAD)
                dve.sem_inc(sems.sum_free, 1)
                for p in range(SLOTS):
                    dve.sem_inc(sems.slot_free[p], 1)
                if messages == "edge":
                    v.memset(buf.edge_a[:, :, H:H + 1], 1.0)
                with dve.Fori(0, NG // SLOTS) as i:
                    for p in range(SLOTS):
                        g = i * SLOTS + p
                        tile, count, before = group_bounds(dve, k, g)
                        dve.wait_ge(sems.rows[p], (i + 1) * GATHERED)
                        dve.sem_inc(sems.seen, 1)
                        by_edge = lambda a, c: a[:, bass.ds(g * G, G)].unsqueeze(2).broadcast_to([P, G, c])
                        if messages == "signed":
                            v.tensor_tensor(buf.edge_a[:, :, 0:D], buf.rows[:, p, :, 0:D], by_edge(k.wpos, D), ALU.mult)
                            v.tensor_tensor(buf.edge_a[:, :, D:2 * D], buf.rows[:, p, :, 0:D], by_edge(k.wneg, D),
                                            ALU.mult).then_inc(made, 1)
                        if messages == "edge":
                            for c, (a, b) in enumerate(CHUNKS):
                                dve.wait_ge(edge_sum, g * NC + c + 1)
                                v.tensor_tensor(buf.edge_b[:, a:b, :], ps_edge[:, a:b, :], buf.rows[:, p, a:b, :],
                                                ALU.add).then_inc(relu_in, 1)
                            v.tensor_copy(buf.edge_a[:, :, H + 1:H + 2], by_edge(k.wpos, 1))
                            v.tensor_copy(buf.edge_a[:, :, H + 2:H + 3], by_edge(k.wneg, 1)).then_inc(weights_made, 1)
                        with dve.Fori(0, count) as w:
                            at = window_tile(k, tile, w)
                            window_targets(k, buf, dve, sems, g, at, (before + w) * 2 + 2)
                            for a, b in CHUNKS:
                                for t in range(a, b):
                                    last = v.tensor_scalar(buf.hot[:, t, :], k.iota[:, :], buf.dst_rel[:, t:t + 1], None,
                                                           ALU.is_equal)
                                last.then_inc(sems.hot_ready, 1)
                            dve.wait_ge(sems.sum_ready, before + w + 1)
                            v.tensor_tensor(k.acc[:, bass.ds(at, 1), 0:cols].rearrange("p a c -> p (a c)"),
                                            k.acc[:, bass.ds(at, 1), 0:cols].rearrange("p a c -> p (a c)"),
                                            total, ALU.add).then_inc(sems.dve_step, 1)
                            dve.wait_ge(sems.dve_step, (before + w) * 2 + 3)
                            dve.sem_inc(sems.sum_free, 1)
                        dve.sem_inc(sems.slot_free[p], 1)

            @block.scalar
            def _(act):
                if messages != "edge":
                    return
                with act.Fori(0, NG // SLOTS) as i:
                    for p in range(SLOTS):
                        g = i * SLOTS + p
                        for c, (a, b) in enumerate(CHUNKS):
                            act.wait_ge(relu_in, g * NC + c + 1)
                            last = nc.scalar.activation(buf.edge_a[:, a:b, 0:H], buf.edge_b[:, a:b, :], ACT.Relu)
                            last.then_inc(made, 1)

            @block.tensor
            def _(pe):
                if messages == "edge":
                    pe.sem_inc(attr_free, SLOTS)
                with pe.Fori(0, NG // SLOTS) as i:
                    for p in range(SLOTS):
                        g = i * SLOTS + p
                        _, count, before = group_bounds(pe, k, g)
                        if messages == "edge":
                            pe.wait_ge(attr_in[p], (i + 1) * 16)
                            for a, b in CHUNKS:
                                for t in range(a, b):
                                    last = nc.tensor.matmul(ps_edge[:, t, :], attr[:, p, t * P:(t + 1) * P],
                                                            k.weight["W1a_edge"][:, :], start=True, stop=True)
                                last.then_inc(edge_sum, 1)
                        if messages == "rows":
                            pe.wait_ge(sems.rows[p], (i + 1) * GATHERED)
                        elif messages == "signed":
                            pe.wait_ge(made, g + 1)
                        else:
                            pe.wait_ge(made, (g + 1) * NC)
                            pe.wait_ge(weights_made, g + 1)
                            pe.sem_inc(attr_free, 1)
                        pe.sem_inc(sems.fence, 1)
                        with pe.Fori(0, count) as w:
                            pe.wait_ge(sems.sum_free, before + w + 1)
                            for c, (a, b) in enumerate(CHUNKS):
                                pe.wait_ge(sems.hot_ready, (before + w) * NC + c + 1)
                                for t in range(a, b):
                                    rhs = buf.rows[:, p, t, 0:width] if messages == "rows" else buf.edge_a[:, t, 0:cols]
                                    last = nc.tensor.matmul(total, buf.hot[:, t, :], rhs,
                                                            start=(t == 0), stop=(t == G - 1))
                            last.then_inc(sems.sum_ready, 1)


def magic_round(v, chain, out, a, scale, shift):
    chain.link(v.tensor_scalar(out, a, scale, shift, ALU.mult, ALU.add))
    chain.link(v.tensor_scalar(out, out, 1.5 * 2.0 ** 23, None, ALU.add))
    chain.link(v.tensor_scalar(out, out, -1.5 * 2.0 ** 23, None, ALU.add))


class Attention:

    def __init__(self, k):
        nc = k.nc
        self.counts = nc.dram_tensor("edge_counts", (NPAD * NQ, QC), FP32, kind="Internal").ap()
        self.marks = nc.dram_tensor("edge_marks", (NPAD * NQ, QC), UINT8, kind="Internal").ap()
        self.s_row = nc.dram_tensor("s_row", (NT, P), FP32, kind="Internal").ap()
        self.ends = nc.dram_tensor("tile_ends", (2, ET), FP32, kind="Internal").ap()
        self.ranges = nc.dram_tensor("tile_ranges", (2, NWIN), FP32, kind="Internal").ap()


def edge_keys(k, att, key_s, key_t, base_s, base_t, ramp, win_bounds):
    nc, d = k.nc, k.dram
    with ExitStack() as ctx, semaphores(nc, "ek") as sem:
        sb = lambda name, shape, dt=FP32: ctx.enter_context(nc.sbuf_tensor("ek_" + name, shape, dt))
        loaded, made, ends_ready, ends_out = sem("loaded"), sem("made"), sem("ends_ready"), sem("ends_out")
        ends_in, ranges_ready, ranges_out, ranges_in = sem("ends_in"), sem("ranges_ready"), sem("ranges_out"), sem("ranges_in")
        step = sem("step")
        rows = ET // 7
        dst_rows, dst_rows_f = sb("dst_rows", [rows, 7, P], INT32), sb("dst_rows_f", [rows, 7, P])
        low, high = sb("low", [rows, 7]), sb("high", [rows, 7])
        all_low, all_high = sb("all_low", [P, ET]), sb("all_high", [P, ET])
        tile_no, tile_no_i = sb("tile_no", [P, ET]), sb("tile_no_i", [P, ET], INT32)
        first_t, first_t_i = sb("first_t", [P, 2]), sb("first_t_i", [P, 1], INT32)
        part, ends = sb("part", [P, ET]), sb("ends", [P, 4])
        pair_i, row = sb("pair_i", [P, 1], INT32), sb("row", [1, 4, NWIN])
        ramp_i, base_i = sb("ramp_i", [P, QC], INT32), sb("base_i", [P, 2, NWIN], INT32)
        hi_i, lo_i = sb("hi_i", [P, ET], INT32), sb("lo_i", [P, ET], INT32)
        hi, lo, q, m = (sb(n, [P, ET]) for n in ("hi", "lo", "q", "m"))

        with nc.Block() as block:
            @block.gpsimd
            def _(pool):
                g = nc.gpsimd
                g.iota(tile_no_i[:, :], pattern=[[1, ET]], base=0, channel_multiplier=0)
                g.iota(first_t_i[:, :], pattern=[[0, 1]], base=0, channel_multiplier=WIN)
                g.iota(ramp_i[:, :], pattern=[[1, QC]], base=0, channel_multiplier=0)
                g.iota(base_i[:, 0, :], pattern=[[-WIN * QW, NWIN]], base=0, channel_multiplier=0)
                g.iota(base_i[:, 1, :], pattern=[[-P, NWIN]], base=0, channel_multiplier=0).then_inc(made, 1)

            @block.sync
            def _(sp):
                sp.dma_start(dst_rows[:, :, :], d["dst_rows"]).then_inc(loaded, 16)
                sp.wait_ge(ends_ready, 1)
                sp.dma_start(att.ends[0, :].rearrange("(p t) -> p t", t=7), low[:, :]).then_inc(ends_out, 16)
                sp.dma_start(att.ends[1, :].rearrange("(p t) -> p t", t=7), high[:, :]).then_inc(ends_out, 16)
                sp.wait_ge(ends_out, 32)
                sp.dma_start(all_low[:, :], att.ends[0, :].partition_broadcast(P)).then_inc(ends_in, 16)
                sp.dma_start(all_high[:, :], att.ends[1, :].partition_broadcast(P)).then_inc(ends_in, 16)
                sp.wait_ge(ranges_ready, 1)
                for j in range(2):
                    sp.dma_start(att.ranges[j, :].rearrange("(p o) -> p o", o=1), ends[:, 2 + j:3 + j])\
                        .then_inc(ranges_out, 16)
                sp.wait_ge(ranges_out, 32)
                sp.dma_start(row[:, 0:2, :], att.ranges.rearrange("(o a) b -> o a b", o=1)).then_inc(ranges_in, 16)

            @block.vector
            def _(dve):
                v, chain = nc.vector, Chain(dve, step)
                dve.wait_ge(made, 1)
                v.tensor_copy(tile_no[:, :], tile_no_i[:, :])
                v.tensor_copy(ramp[:, :], ramp_i[:, :])
                v.tensor_copy(base_s[:, :], base_i[:, 0, :])
                v.tensor_copy(base_t[:, :], base_i[:, 1, :])
                chain.link(v.tensor_copy(first_t[:, 0:1], first_t_i[:, :]))
                chain.link(v.tensor_scalar(first_t[:, 1:2], first_t[:, 0:1], WIN - 1.0, None, ALU.add))
                dve.wait_ge(loaded, 16)
                chain.link(v.tensor_copy(dst_rows_f[:, :, :], dst_rows[:, :, :]))
                v.tensor_reduce(low[:, :], dst_rows_f[:, :, :], AX.X, ALU.min)
                v.tensor_reduce(high[:, :], dst_rows_f[:, :, :], AX.X, ALU.max).then_inc(ends_ready, 1)
                v.memset(key_s[:, ET:], -1.0)
                v.memset(key_t[:, ET:], -1.0)
                chain.link(v.tensor_scalar(hi_i[:, :], k.src_idx[:, 0:ET], 7, None, ALU.arith_shift_right))
                chain.link(v.tensor_scalar(lo_i[:, :], k.src_idx[:, 0:ET], P - 1, None, ALU.bitwise_and))
                chain.link(v.tensor_copy(hi[:, :], hi_i[:, :]))
                chain.link(v.tensor_copy(lo[:, :], lo_i[:, :]))
                magic_round(v, chain, q[:, :], hi[:, :], 1.0 / QW, -0.4)
                chain.link(v.scalar_tensor_tensor(m[:, :], q[:, :], -float(QW), hi[:, :], ALU.mult, ALU.add))
                chain.link(v.scalar_tensor_tensor(q[:, :], m[:, :], float(WIN * QW), q[:, :], ALU.mult, ALU.add))
                chain.link(v.scalar_tensor_tensor(key_s[:, 0:ET], k.dst_f[:, :], float(QW), q[:, :], ALU.mult, ALU.add))
                magic_round(v, chain, m[:, :], k.dst_f[:, :], 1.0 / WIN, -0.48)
                chain.link(v.scalar_tensor_tensor(key_t[:, 0:ET], m[:, :], float(P), lo[:, :], ALU.mult, ALU.add))
                dve.wait_ge(ends_in, 32)
                chain.link(v.tensor_scalar(part[:, :], all_high[:, :], first_t[:, 0:1], float(2 * ET), ALU.is_lt, ALU.mult))
                chain.link(v.tensor_tensor(part[:, :], part[:, :], tile_no[:, :], ALU.add))
                chain.link(v.tensor_reduce(ends[:, 0:1], part[:, :], AX.X, ALU.min))
                chain.link(v.tensor_scalar(part[:, :], all_low[:, :], first_t[:, 1:2], -float(2 * ET), ALU.is_gt, ALU.mult))
                chain.link(v.tensor_tensor(part[:, :], part[:, :], tile_no[:, :], ALU.add))
                chain.link(v.tensor_reduce(ends[:, 1:2], part[:, :], AX.X, ALU.max))
                chain.link(v.tensor_scalar(ends[:, 2:3], ends[:, 0:1], float(ET), None, ALU.min))
                chain.link(v.tensor_tensor(ends[:, 3:4], ends[:, 1:2], ends[:, 2:3], ALU.subtract))
                chain.link(v.tensor_scalar(ends[:, 3:4], ends[:, 3:4], 2.0, 4.0, ALU.add, ALU.max))
                chain.link(v.tensor_copy(pair_i[:, :], ends[:, 3:4]))
                chain.link(v.tensor_scalar(pair_i[:, :], pair_i[:, :], 1, None, ALU.arith_shift_right))
                v.tensor_copy(ends[:, 3:4], pair_i[:, :]).then_inc(ranges_ready, 1)
                dve.wait_ge(ranges_in, 16)
                v.memset(row[:, 3, :], 1.0)
                v.tensor_copy(win_bounds[:, 0:NWIN], row[:, 0, :])
                chain.link(v.tensor_scalar(win_bounds[:, NWIN:2 * NWIN], row[:, 1, :], -1.0, None, ALU.add))
                chain.link(v.tensor_tensor_scan(row[:, 2, :], row[:, 3, :], row[:, 1, :], 0.0, ALU.mult, ALU.add))
                chain.link(v.tensor_tensor(row[:, 2, :], row[:, 2, :], row[:, 1, :], ALU.subtract))
                chain.link(v.tensor_copy(win_bounds[:, 2 * NWIN:], row[:, 2, :]))


def build_counts(k, att):
    nc = k.nc
    with ExitStack() as ctx:
        sb = lambda name, shape, dt=FP32: ctx.enter_context(nc.sbuf_tensor("bc_" + name, shape, dt))
        key_s, key_t = sb("key_s", [P, ET + PAD_TILES]), sb("key_t", [P, ET + PAD_TILES])
        base_s, base_t = sb("base_s", [P, NWIN]), sb("base_t", [P, NWIN])
        ramp, win_bounds = sb("ramp", [P, QC], FP16), sb("win_bounds", [1, 3 * NWIN], INT32)
        edge_keys(k, att, key_s, key_t, base_s, base_t, ramp, win_bounds)

        sem = ctx.enter_context(semaphores(nc, "bc"))
        hot_ready, hot_used, summed, counts_ready = sem("hot_ready"), sem("hot_used"), sem("summed"), sem("counts_ready")
        marks_ready, fence = sem("marks_ready"), sem("fence")
        counts_out = [sem(f"counts_out{y}") for y in range(2)]
        marks_out = [sem(f"marks_out{y}") for y in range(2)]
        evacuated = sem("evacuated")
        hot_s, hot_t = sb("hot_s", [P, BUILD, QC], FP16), sb("hot_t", [P, BUILD, P], FP16)
        counts, marks = sb("counts", [WIN * QW, 2, QC]), sb("marks", [WIN * QW, 2, QC], UINT8)
        ps = [k.psum_cols(4 * y, P, QC) for y in range(2)]
        ROWS = WIN * QW

        def window_range(eng, j):
            first = eng.value_load(win_bounds[0:1, bass.ds(j, 1)], min_val=0, max_val=ET)
            steps = eng.value_load(win_bounds[0:1, bass.ds(j + NWIN, 1)], min_val=1, max_val=ET // BUILD)
            before = eng.value_load(win_bounds[0:1, bass.ds(j + 2 * NWIN, 1)], min_val=0, max_val=NWIN * ET // BUILD)
            return first, steps, before

        with nc.Block() as block:
            @block.vector
            def _(dve):
                v = nc.vector

                def one_hots(j, first, n):
                    for u in range(BUILD):
                        t = nc.s_assert_within(first + u, 0, ET + PAD_TILES - 1,
                                               skip_runtime_bounds_check_because="no range ends behind the padding")
                        dve.wait_ge(hot_used, n * BUILD + u + 1)
                        column = lambda a, at: a[:, bass.ds(at, 1)]
                        v.tensor_scalar(hot_s[:, u, :], ramp[:, :], column(key_s, t), column(base_s, j),
                                        ALU.subtract, ALU.is_equal)
                        v.tensor_scalar(hot_t[:, u, :], ramp[:, 0:P], column(key_t, t), column(base_t, j),
                                        ALU.subtract, ALU.is_equal).then_inc(hot_ready, 1)

                dve.sem_inc(hot_used, BUILD)
                with dve.Fori(0, NWIN // 2) as i:
                    for y in range(2):
                        j = i * 2 + y
                        first, steps, before = window_range(dve, j)
                        one_hots(j, first, before)
                        with dve.Fori(0, steps) as w:
                            one_hots(j, first + (w + 1) * BUILD, before + w + 1)

            @block.tensor
            def _(pe):
                def products(y, n, start):
                    for u in range(BUILD):
                        pe.wait_ge(hot_ready, n * BUILD + u + 1)
                        for m in range(QW):
                            last = nc.tensor.matmul(ps[y][:, m * P:(m + 1) * P], hot_s[:, u, m * WIN * QW:m * WIN * QW + P],
                                                    hot_t[:, u, :], start=start and u == 0 and m in (0, QW - 1),
                                                    stop=True, skip_group_check=True)
                        last.then_inc(hot_used, 1)

                with pe.Fori(0, NWIN // 2) as i:
                    for y in range(2):
                        _, steps, before = window_range(pe, i * 2 + y)
                        pe.wait_ge(evacuated, i * 2 + y + 1)
                        pe.sem_inc(fence, 1)
                        products(y, before, True)
                        with pe.Fori(0, steps) as w:
                            products(y, before + w + 1, False)
                        pe.wait_ge(hot_used, (before + steps + 1) * BUILD + BUILD)
                        pe.sem_inc(summed, 1)

            @block.scalar
            def _(act):
                act.sem_inc(evacuated, 2)
                with act.Fori(0, NWIN // 2) as i:
                    for y in range(2):
                        act.wait_ge(summed, i * 2 + y + 1)
                        act.wait_ge(counts_out[y], i * 16 + 16)
                        act.wait_ge(marks_ready, i * 2 + y + 1)
                        nc.scalar.activation(counts[:, y, :], ps[y][0:ROWS, :], ACT.Copy).then_inc(counts_ready, 1)
                        act.wait_ge(counts_ready, i * 2 + y + 1)
                        act.sem_inc(evacuated, 1)

            @block.gpsimd
            def _(pool):
                pool.sem_inc(marks_ready, 2)
                with pool.Fori(0, NWIN // 2) as i:
                    for y in range(2):
                        pool.wait_ge(counts_ready, i * 2 + y + 1)
                        pool.wait_ge(marks_out[y], i * 16 + 16)
                        pool.sem_inc(fence, 1)
                        nc.gpsimd.tensor_scalar(marks[:, y, :], counts[:, y, :], 1.0, None, ALU.min)\
                            .then_inc(marks_ready, 1)

            @block.sync
            def _(sp):
                for y in range(2):
                    sp.sem_inc(counts_out[y], 16)
                    sp.sem_inc(marks_out[y], 16)
                with sp.Fori(0, NWIN // 2) as i:
                    for y in range(2):
                        rows = bass.ds((i * 2 + y) * ROWS, ROWS)
                        sp.wait_ge(counts_ready, i * 2 + y + 1)
                        sp.dma_start(att.counts[rows, :], counts[:, y, :]).then_inc(counts_out[y], 16)
                        sp.wait_ge(marks_ready, i * 2 + y + 3)
                        sp.dma_start(att.marks[rows, :], marks[:, y, :]).then_inc(marks_out[y], 16)
                for y in range(2):
                    sp.wait_ge(counts_out[y], 16 * (NWIN // 2) + 16)
                    sp.wait_ge(marks_out[y], 16 * (NWIN // 2) + 16)


def attention_layer(k, tag, att):
    nc = k.nc
    MARK_SLOTS = 4
    PS_SETS = 3
    with ExitStack() as ctx, semaphores(nc, tag) as sem:
        sb = lambda name, shape, dt=FP32: ctx.enter_context(nc.sbuf_tensor(f"{tag}_{name}", shape, dt))
        s_all = sb("s_all", [P, NPAD])
        marks = sb("marks", [P, MARK_SLOTS, NPAD], UINT8)
        s_max, e_top, e_max = sb("s_max", [P, NT]), sb("e_top", [P, NT]), sb("e_max", [P, NT])
        bias_1, bias_2 = sb("bias_1", [P, NT]), sb("bias_2", [P, NT])
        counts, exp_1, exp_2 = sb("counts", [P, NQ, QC]), sb("exp_1", [P, NQ, QC]), sb("exp_2", [P, NQ, QC])
        probs, probs_t = sb("probs", [P, NQ, QC]), sb("probs_t", [P, NQ, QC])
        ps_turn = [k.psum_cols(2 * y, P, QC) for y in range(PS_SETS)]
        total = k.psum[:, 6, 0:D + 1]
        s_in, marks_used, step, ready = sem("s_in"), sem("marks_used"), sem("step"), sem("ready")
        marks_in = [sem(f"marks_in{y}") for y in range(MARK_SLOTS)]
        counts_in = [sem(f"counts_in{c}") for c in range(NQ)]
        exps, greater, masked, turned = sem("exps"), sem("greater"), sem("masked"), sem("turned")
        copied, used, sum_ready, sum_free, fence = (sem(n) for n in ("copied", "used", "sum_ready", "sum_free", "fence"))

        def back(d, c, lag):
            return (d, c - lag) if c >= lag else (d - 1, c - lag + NQ)

        with nc.Block() as block:
            @block.sync
            def _(sp):
                sp.dma_start(s_all[:, :], att.s_row.rearrange("t p -> (t p)").partition_broadcast(P)).then_inc(s_in, 16)
                tile_marks = att.marks.rearrange("(t p q) c -> t p (q c)", p=P, q=NQ)
                for t in range(NT):
                    if t >= MARK_SLOTS:
                        sp.wait_ge(marks_used, t - MARK_SLOTS + 1)
                    sp.dma_start(marks[:, t % MARK_SLOTS, :], tile_marks[t, :, :])\
                        .then_inc(marks_in[t % MARK_SLOTS], 16)
                tile_counts = att.counts.rearrange("(t p q) c -> p t q c", p=P, q=NQ)
                with sp.Fori(0, NT) as d:
                    for c in range(NQ):
                        sp.wait_ge(masked, d * NQ + c + 1)
                        sp.dma_start(counts[:, c, :], tile_counts[:, bass.ds(d, 1), c, :]
                                     .rearrange("p a c -> p (a c)")).then_inc(counts_in[c], 16)

            @block.vector
            def _(dve):
                v, chain = nc.vector, Chain(dve, step)
                for s in (masked, used):
                    dve.sem_inc(s, NQ)
                dve.sem_inc(sum_free, 1)
                dve.sem_inc(turned, NQ)
                dve.wait_ge(s_in, 16)
                for t in range(NT):
                    dve.wait_ge(marks_in[t % MARK_SLOTS], 16 * (t // MARK_SLOTS + 1))
                    v.tensor_tensor_reduce(out=(probs, probs_t)[t % 2][:, :, :].rearrange("p q c -> p (q c)"),
                                           in0=marks[:, t % MARK_SLOTS, :], in1=s_all[:, :], scale=1.0, scalar=0.0,
                                           op0=ALU.mult, op1=ALU.max, accum_out=s_max[:, t:t + 1]).then_inc(marks_used, 1)
                    if t >= 1:
                        dve.wait_ge(marks_used, t)
                dve.wait_ge(marks_used, NT)
                chain.link(v.tensor_tensor(e_top[:, :], s_max[:, :], k.d_low[:, :], ALU.add))
                chain.link(v.scalar_tensor_tensor(e_max[:, :], e_top[:, :], SLOPE, e_top[:, :], ALU.mult, ALU.max))
                v.tensor_tensor(bias_1[:, :], k.d_low[:, :], e_max[:, :], ALU.subtract)
                v.scalar_tensor_tensor(bias_2[:, :], k.d_low[:, :], SLOPE, e_max[:, :], ALU.mult, ALU.subtract)\
                    .then_inc(ready, 1)

                def greatest(d, c):
                    dve.wait_ge(exps, d * NQ + c + 1)
                    v.tensor_tensor(exp_1[:, c, :], exp_1[:, c, :], exp_2[:, c, :], ALU.max).then_inc(greater, 1)

                def mask(d, c):
                    dve.wait_ge(greater, d * NQ + c + 1)
                    dve.wait_ge(counts_in[c], d * 16 + 16)
                    dve.wait_ge(turned, d * NQ + c + 1)
                    v.scalar_tensor_tensor(probs[:, c, :], exp_1[:, c, :], 1.0, counts[:, c, :], ALU.min, ALU.mult)\
                        .then_inc(masked, 1)

                def store(d):
                    dve.wait_ge(sum_ready, d + 1)
                    v.tensor_copy(k.acc[:, bass.ds(d, 1), 0:D + 1].rearrange("p a c -> p (a c)"), total)\
                        .then_inc(sum_free, 1)

                def tile(d, first=False):
                    for c in range(NQ):
                        greatest(d, c)
                        if c >= 1 or not first:
                            mask(*back(d, c, 1))
                        if c == 2 and not first:
                            store(d - 1)

                tile(0, True)
                with dve.Fori(1, NT) as d:
                    tile(d)
                mask(NT - 1, NQ - 1)
                store(NT - 1)

            @block.scalar
            def _(act):
                def exponentials(d, c):
                    act.wait_ge(masked, d * NQ + c + 1)
                    act.sem_inc(fence, 1)
                    nc.scalar.activation(exp_1[:, c, :], s_all[:, c * QC:(c + 1) * QC], ACT.Exp,
                                         bias=bias_1[:, bass.ds(d, 1)])
                    nc.scalar.activation(exp_2[:, c, :], s_all[:, c * QC:(c + 1) * QC], ACT.Exp,
                                         bias=bias_2[:, bass.ds(d, 1)], scale=SLOPE).then_inc(exps, 1)

                def copy(d, c):
                    act.wait_ge(turned, d * NQ + c + 1 + NQ)
                    act.wait_ge(used, d * NQ + c + 1)
                    nc.scalar.activation(probs_t[:, c, :], ps_turn[c % PS_SETS], ACT.Copy).then_inc(copied, 1)

                act.wait_ge(s_in, 16)
                act.wait_ge(ready, 1)
                act.sem_inc(copied, 2)

                def tile(d, first=False):
                    for c in range(NQ):
                        exponentials(d, c)
                        if c >= 3 or not first:
                            copy(*back(d, c, 3))

                tile(0, True)
                with act.Fori(1, NT) as d:
                    tile(d)
                for c in range(2, NQ):
                    copy(NT - 1, c)

            @block.tensor
            def _(pe):
                LEFT = (1, 2, 1, 3, 4)

                def turn(d, c):
                    pe.wait_ge(masked, d * NQ + c + 1 + NQ)
                    pe.wait_ge(copied, d * NQ + LEFT[c])
                    for b in range(QW):
                        last = nc.tensor.transpose(ps_turn[c % PS_SETS][:, b * P:(b + 1) * P],
                                                   probs[:, c, b * P:(b + 1) * P], k.ident[:, :])
                    last.then_inc(turned, 1)

                def add_up(d, c):
                    pe.wait_ge(copied, d * NQ + c + 1 + 2)
                    if c == 0:
                        pe.wait_ge(sum_free, d + 1)
                    for b in range(QW):
                        last = nc.tensor.matmul(total, probs_t[:, c, b * P:(b + 1) * P], k.z[:, c * QW + b, 0:D + 1],
                                                start=(c == 0 and b == 0), stop=(c == NQ - 1 and b == QW - 1))
                    last.then_inc(used, 1)
                    if c == NQ - 1:
                        pe.wait_ge(used, d * NQ + NQ + NQ)
                        pe.sem_inc(sum_ready, 1)

                def tile(d, first=False):
                    for c in range(NQ):
                        turn(d, c)
                        if c >= 2 or not first:
                            add_up(*back(d, c, 2))

                tile(0, True)
                with pe.Fori(1, NT) as d:
                    tile(d)
                for c in (NQ - 2, NQ - 1):
                    add_up(NT - 1, c)


def over_columns(a, count):
    return a.unsqueeze(2).broadcast_to([a.shape[0], a.shape[1], count])


def over_tiles(a, tiles):
    return a.unsqueeze(1).broadcast_to([a.shape[0], tiles, a.shape[1]])


class NodePhase:

    def __init__(self, k, tag):
        self.k, self.tag = k, tag
        self.before = self.load = self.store = self.after = None
        self.w_mid = self.w_out = self.mid_bias = None
        self.kdim = self.cols = 0
        self.roots_before = self.roots_after = 0
        self.tables = []
        self.step_table = None
        self.least = False
        self.global_bias = False

    def build(self):
        k, nc, tag = self.k, self.k.nc, self.tag
        with semaphores(nc, tag) as sem:
            fence = sem("fence")
            step, staged, turned, copied = sem("step"), sem("staged"), sem("turned"), sem("copied")
            mid_sum, mid_ready, out_sum, table_free = sem("mid_sum"), sem("mid_ready"), sem("out_sum"), sem("table_free")
            self.inner = sem("inner")
            self.root_in, self.root_out = sem("root_in"), sem("root_out")
            self.fold_in, self.fold_out = sem("fold_in"), sem("fold_out")
            table_ready, written, stored, ready = sem("table_ready"), sem("written"), sem("stored"), sem("ready")
            ps_t = k.psum_cols(0, max(self.kdim, 1), NB * P)
            ps_mid = k.psum_cols(2, H, NB * P)
            width = P if self.cols <= P else 512
            ps_out = k.psum_cols(3 if width > P else 4, P, NB * width).rearrange("p (t c) -> p t c", c=width)

            with nc.Block() as block:
                @block.vector
                def _(dve):
                    chain = Chain(dve, step)
                    if self.before:
                        self.before(dve, chain)
                    if self.load:
                        with dve.Fori(0, NSTEP) as i:
                            self.load(i).then_inc(staged, 1)
                            dve.wait_ge(out_sum, i + 1)
                            if self.step_table:
                                dve.wait_ge(table_free, i + 1)
                            self.store(i, ps_out[:, :, 0:self.cols]).then_inc(stored, 1)
                            dve.wait_ge(stored, i + 1)
                    if self.after:
                        self.after(dve, chain)
                    v_done = nc.vector.memset(k.per_node[:, 3, 0:1], 0.0)
                    v_done.then_inc(table_ready, 1)

                @block.tensor
                def _(pe):
                    if self.global_bias:
                        nc.tensor.matmul(k.psum[:, 7, 0:1], k.weight["W2a_u"][:, :], k.weight["c_u"][:, :],
                                         start=True, stop=True).then_inc(self.fold_out, 1)
                    if self.load:
                        with pe.Fori(0, NSTEP) as i:
                            pe.wait_ge(staged, i + 1)
                            pe.sem_inc(fence, 1)
                            for j in range(NB):
                                last = nc.tensor.transpose(ps_t[:, j * P:(j + 1) * P],
                                                           k.node_in[:, j, 0:self.kdim], k.ident[:, :])
                            last.then_inc(turned, 1)
                            pe.wait_ge(copied, i + 1)
                            pe.sem_inc(fence, 1)
                            turned_in = k.node_inT
                            if self.w_mid is not None:
                                for a, b in ((0, 512), (512, NB * P)):
                                    last = nc.tensor.matmul(ps_mid[:, a:b], self.w_mid, k.node_inT[0:self.kdim, a:b],
                                                            start=True, stop=True)
                                last.then_inc(mid_sum, 1)
                                pe.wait_ge(mid_ready, i + 1)
                                turned_in = k.node_midT
                            rows = self.w_out.shape[0]
                            for j in range(NB):
                                last = nc.tensor.matmul(ps_out[:, j, 0:self.cols], turned_in[0:rows, j * P:(j + 1) * P],
                                                        self.w_out, start=True, stop=True)
                            last.then_inc(out_sum, 1)
                    if self.least:
                        pe.wait_ge(self.fold_in, 1)
                        nc.tensor.transpose(k.psum[0:1, 7, 0:P], k.per_node[:, 0, 0:1], k.ident[:, :])\
                            .then_inc(self.fold_out, 1)
                        pe.wait_ge(self.fold_in, 2)
                        nc.tensor.matmul(k.psum[:, 7, 256:257], k.ones[0:1, :], k.per_node[0:1, 0, 1:2],
                                         start=True, stop=True).then_inc(self.fold_out, 1)
                        pe.wait_ge(self.fold_in, 3)
                        nc.tensor.transpose(k.psum[0:NT, 6, 0:P], k.z[:, :, D + 1], k.ident[:, :])\
                            .then_inc(self.fold_out, 1)

                @block.scalar
                def _(act):
                    roots = 0
                    for _ in range(self.roots_before):
                        roots += 1
                        act.wait_ge(self.root_in, roots)
                        nc.scalar.activation(k.std[:, :, :], k.var[:, :, :], ACT.Sqrt).then_inc(self.root_out, 1)
                    if self.load:
                        with act.Fori(0, NSTEP) as i:
                            act.wait_ge(turned, i + 1)
                            nc.scalar.activation(k.node_inT[0:self.kdim, :], ps_t[:, :], ACT.Copy).then_inc(copied, 1)
                            if self.w_mid is not None:
                                act.wait_ge(mid_sum, i + 1)
                                nc.scalar.activation(k.node_midT[:, :], ps_mid[:, :], ACT.Relu, bias=self.mid_bias)\
                                    .then_inc(mid_ready, 1)
                    for _ in range(self.roots_after):
                        roots += 1
                        act.wait_ge(self.root_in, roots)
                        nc.scalar.activation(k.std[:, :, :], k.var[:, :, :], ACT.Sqrt).then_inc(self.root_out, 1)

                @block.sync
                def _(sp):
                    if self.step_table:
                        to, source = self.step_table
                        sp.sem_inc(table_free, 1)
                        with sp.Fori(0, NSTEP) as i:
                            sp.wait_ge(stored, i + 1)
                            sp.dma_start(to[:, bass.ds(i * NB, NB), :], source).then_inc(written, 16)
                            sp.wait_ge(written, (i + 1) * 16)
                            sp.sem_inc(table_free, 1)
                    if self.tables:
                        sp.wait_ge(table_ready, 1)
                        for to, source in self.tables:
                            sp.dma_start(to, source).then_inc(written, 16)
                        sp.wait_ge(written, 16 * len(self.tables))


def root(phase, dve):
    dve.sem_inc(phase.root_in, 1)


def layer_norm(phase, dve, chain, roots):
    k, v = phase.k, phase.k.nc.vector
    mean, spread = k.per_node[:, 0, :], k.per_node[:, 1, :]
    chain.link(v.tensor_reduce(mean, k.h[:, :, :], AX.X, ALU.add))
    chain.link(v.tensor_scalar(mean, mean, -1.0 / D, None, ALU.mult))
    chain.link(v.tensor_tensor(k.h[:, :, :], k.h[:, :, :], over_columns(mean, D), ALU.add))
    chain.link(v.tensor_tensor(k.big[:, :, 0:D], k.h[:, :, :], k.h[:, :, :], ALU.mult))
    chain.link(v.tensor_reduce(spread, k.big[:, :, 0:D], AX.X, ALU.add))
    v.memset(k.var[:, :, 1:2], 1.0)
    v.tensor_scalar(k.var[:, :, 0], spread, 1.0 / D, EPS, ALU.mult, ALU.add).then_inc(phase.root_in, 1)
    dve.wait_ge(phase.root_out, roots)
    chain.link(v.reciprocal(spread, k.std[:, :, 0]))
    chain.link(v.tensor_tensor(k.x[:, :, :], k.h[:, :, :], over_columns(spread, D), ALU.mult))


def gat_finish(k, chain, relu):
    v = k.nc.vector
    rest = k.per_node[:, 0, :]
    chain.link(v.tensor_scalar(rest, k.acc[:, :, D], 1e-30, None, ALU.max))
    chain.link(v.reciprocal(rest, rest))
    chain.link(v.tensor_tensor(k.h[:, :, :], k.acc[:, :, 0:D], over_columns(rest, D), ALU.mult))
    if relu:
        chain.link(v.tensor_scalar(k.h[:, :, :], k.h[:, :, :], 0.0, None, ALU.max))


def attention_nodes(k, layer, att):
    phase, v = NodePhase(k, f"gt{layer}"), k.nc.vector
    w = k.weight
    source = k.x if layer == 0 else k.h
    phase.kdim, phase.cols, phase.w_out = D, D, w[f"W0{layer}"][:, :]
    phase.least = True
    if layer:
        phase.before = lambda dve, chain: gat_finish(k, chain, True)
    phase.load = lambda i: v.tensor_copy(k.node_in[:, :, 0:D], source[:, bass.ds(i * NB, NB), :])
    phase.store = lambda i, ps: v.tensor_tensor(k.z[:, bass.ds(i * NB, NB), 0:D], ps,
                                                over_tiles(w[f"b_0{layer}"][:, :], NB), ALU.add)

    def after(dve, chain):
        s, d = k.per_node[:, 1, :], k.per_node[:, 2, :]
        z = k.z[:, :, 0:D]
        v.memset(k.z[:, :, D:D + 1], 1.0)
        chain.link(v.tensor_tensor(k.big[:, :, 0:D], z, over_tiles(w[f"a_src{layer}"][:, :], NT), ALU.mult))
        v.tensor_tensor(k.big[:, :, D:2 * D], z, over_tiles(w[f"a_dst{layer}"][:, :], NT), ALU.mult)
        chain.link(v.tensor_reduce(s, k.big[:, :, 0:D], AX.X, ALU.add))
        chain.link(v.tensor_reduce(d, k.big[:, :, D:2 * D], AX.X, ALU.add))
        v.tensor_reduce(k.per_node[:, 0, 0:1], s, AX.X, ALU.min).then_inc(phase.fold_in, 1)
        dve.wait_ge(phase.fold_out, 1)
        v.tensor_reduce(k.per_node[0:1, 0, 1:2], k.psum[0:1, 7, 0:P], AX.X, ALU.min).then_inc(phase.fold_in, 1)
        dve.wait_ge(phase.fold_out, 2)
        chain.link(v.tensor_scalar(k.per_node[:, 0, 2:3], k.psum[:, 7, 256:257], -1.0, None, ALU.add))
        low = k.per_node[:, 0, 2:3]
        v.tensor_scalar(k.z[:, :, D + 1], s, low, None, ALU.subtract)
        chain.link(v.tensor_scalar(k.d_low[:, :], d, w[f"b_att{layer}"][:, :], low, ALU.add, ALU.add))
        dve.sem_inc(phase.fold_in, 1)
        dve.wait_ge(phase.fold_out, 3)
        v.tensor_copy(k.s_turned[:, :], k.psum[0:NT, 6, 0:P])

    phase.after = after
    phase.tables = [(att.s_row, k.s_turned[:, :])]
    phase.build()


def edge_table(k, table):
    phase, v = NodePhase(k, "et"), k.nc.vector
    phase.kdim, phase.cols, phase.w_out = D, H, k.weight["W1a_node"][:, :]
    phase.roots_before = 1

    def before(dve, chain):
        gat_finish(k, chain, False)
        chain.link(v.tensor_tensor(k.h[:, :, :], k.h[:, :, :], k.x[:, :, :], ALU.add))
        layer_norm(phase, dve, chain, 1)

    phase.before = before
    phase.load = lambda i: v.tensor_copy(k.node_in[:, :, 0:D], k.x[:, bass.ds(i * NB, NB), :])
    phase.store = lambda i, ps: v.tensor_tensor(k.table[:, bass.ds(i * NB, NB), :], ps,
                                                over_tiles(k.weight["b_1a"][:, :], NB), ALU.add)
    phase.tables = [(table.rearrange("(t p) f -> p t f", p=P), k.table[:, :, :])]
    phase.build()


def edge_mean(k):
    phase, v = NodePhase(k, "em"), k.nc.vector
    phase.kdim, phase.cols, phase.w_out = H, D, k.weight["W1b"][:, :]
    phase.roots_before = 1
    share, any_edge = k.per_node[:, 1, :], k.per_node[:, 2, :]

    def before(dve, chain):
        chain.link(v.tensor_scalar(share, k.acc[:, :, H], 1.0, None, ALU.max))
        chain.link(v.reciprocal(share, share))
        v.tensor_scalar(any_edge, k.acc[:, :, H], 1.0, None, ALU.min)
        v.tensor_copy(k.big[:, :, 0:D], k.x[:, :, :])
        chain.link(v.tensor_scalar(k.var[:, :, :], k.acc[:, :, H + 1:H + 3], 1.0, None, ALU.add))
        dve.sem_inc(phase.root_in, 1)
        dve.wait_ge(phase.root_out, 1)
        chain.link(v.reciprocal(k.dinv[:, :, :], k.std[:, :, :]))

    def store(i, ps):
        mean = k.big[:, bass.ds(i * NB, NB), D:2 * D]
        k.nc.vector.tensor_tensor(k.node_out[:, :, :], over_tiles(k.weight["b_1b"][:, :], NB),
                                  over_columns(k.per_node[:, 2, bass.ds(i * NB, NB)], D), ALU.mult)\
            .then_inc(phase.inner, 1)
        k.nc.vector.wait_ge(phase.inner, i + 1)
        return v.tensor_tensor(mean, ps, k.node_out[:, :, :], ALU.add)

    phase.before, phase.store = before, store
    phase.load = lambda i: v.tensor_tensor(k.node_in[:, :, :], k.acc[:, bass.ds(i * NB, NB), 0:H],
                                           over_columns(k.per_node[:, 1, bass.ds(i * NB, NB)], H), ALU.mult)
    phase.build()


def node_mlp(k):
    phase, v = NodePhase(k, "nm"), k.nc.vector
    phase.kdim, phase.cols = 2 * D, D
    phase.w_mid, phase.w_out = k.weight["W2a"][:, :], k.weight["W2b"][:, :]
    phase.mid_bias = k.per_node[:, 3, 1:2]
    phase.global_bias, phase.roots_after = True, 1

    def before(dve, chain):
        dve.wait_ge(phase.fold_out, 1)
        chain.link(v.tensor_tensor(k.per_node[:, 3, 1:2], k.psum[:, 7, 0:1], k.weight["c_2a"][:, :], ALU.add))

    def after(dve, chain):
        chain.link(v.tensor_tensor(k.h[:, :, :], k.h[:, :, :], over_tiles(k.weight["b_2b"][:, :], NT), ALU.add))
        layer_norm(phase, dve, chain, 1)

    phase.before, phase.after = before, after
    phase.load = lambda i: v.tensor_copy(k.node_in[:, :, :], k.big[:, bass.ds(i * NB, NB), :])
    phase.store = lambda i, ps: v.tensor_tensor(k.h[:, bass.ds(i * NB, NB), :], ps,
                                                k.x[:, bass.ds(i * NB, NB), :], ALU.add)
    phase.build()


def relation_table(k, table):
    phase, v = NodePhase(k, "rt"), k.nc.vector
    k.wide_table = k.big[:, 0:2 * RELS * D * NB // (2 * H), :].rearrange("p t c -> p (t c)")\
        .rearrange("p (t c) -> p t c", c=RELS * D)
    phase.kdim, phase.cols, phase.w_out = D, RELS * D, k.weight["Wrel"][:, :]
    phase.load = lambda i: v.tensor_copy(k.node_in[:, :, 0:D], k.x[:, bass.ds(i * NB, NB), :])
    phase.store = lambda i, ps: v.tensor_copy(k.wide_table[:, :, :], ps)
    phase.step_table = (table.rearrange("(t p r) f -> p t (r f)", p=P, r=RELS), k.wide_table[:, :, :])
    phase.build()


def signed_table(k, table):
    phase, v = NodePhase(k, "st"), k.nc.vector
    phase.kdim, phase.cols, phase.w_out = D, D, k.weight["Wself"][:, :]
    phase.roots_after = 1
    phase.load = lambda i: v.tensor_copy(k.node_in[:, :, 0:D], k.x[:, bass.ds(i * NB, NB), :])
    phase.store = lambda i, ps: v.tensor_tensor(k.h[:, bass.ds(i * NB, NB), :], ps,
                                                k.acc[:, bass.ds(i * NB, NB), 0:D], ALU.add)

    def after(dve, chain):
        chain.link(v.scalar_tensor_tensor(k.h[:, :, :], k.h[:, :, :], 0.0, k.x[:, :, :], ALU.max, ALU.add))
        layer_norm(phase, dve, chain, 1)
        for j in range(2):
            chain.link(v.tensor_tensor(k.table[:, :, j * D:(j + 1) * D], k.x[:, :, :],
                                       over_columns(k.dinv[:, :, j], D), ALU.mult))

    phase.after = after
    phase.tables = [(table.rearrange("(t p r) f -> p t (r f)", p=P, r=2), k.table[:, :, :])]
    phase.build()


def gcn_sum(k, chain):
    v = k.nc.vector
    chain.link(v.tensor_tensor(k.acc[:, :, 0:H], k.acc[:, :, 0:H], k.table[:, :, :], ALU.add))
    chain.link(v.tensor_tensor(k.acc[:, :, 0:D], k.acc[:, :, 0:D], over_columns(k.dinv[:, :, 0], D), ALU.mult))
    chain.link(v.tensor_scalar(k.per_node[:, 0, :], k.dinv[:, :, 1], -1.0, None, ALU.mult))
    chain.link(v.tensor_tensor(k.acc[:, :, D:H], k.acc[:, :, D:H], over_columns(k.per_node[:, 0, :], D), ALU.mult))


def gcn_mid(k, table):
    phase, v = NodePhase(k, "gm"), k.nc.vector
    phase.kdim, phase.cols = 2 * D, 2 * D
    phase.w_mid, phase.w_out = k.weight["W3a"][:, :], k.weight["W3b"][:, :]
    phase.mid_bias = k.per_node[:, 3, 1:2]

    def before(dve, chain):
        gcn_sum(k, chain)
        chain.link(v.tensor_tensor(k.per_node[:, 3, 1:2], k.weight["c_3p"][:, :], k.weight["c_3n"][:, :],
                                   ALU.subtract))

    def after(dve, chain):
        for j in range(2):
            part = k.table[:, :, j * D:(j + 1) * D]
            chain.link(v.tensor_tensor(part, part, over_columns(k.dinv[:, :, j], D), ALU.mult))

    phase.before, phase.after = before, after
    phase.load = lambda i: v.tensor_copy(k.node_in[:, :, :], k.acc[:, bass.ds(i * NB, NB), 0:H])
    phase.store = lambda i, ps: v.tensor_copy(k.table[:, bass.ds(i * NB, NB), :], ps)
    phase.tables = [(table.rearrange("(t p r) f -> p t (r f)", p=P, r=2), k.table[:, :, :])]
    phase.build()


def gcn_finish(k, out):
    phase, v = NodePhase(k, "gf"), k.nc.vector
    phase.roots_after = 1

    def after(dve, chain):
        gcn_sum(k, chain)
        chain.link(v.tensor_tensor(k.h[:, :, :], k.acc[:, :, 0:D], k.acc[:, :, D:H], ALU.add))
        bias = k.node_out[:, 0, :]
        chain.link(v.tensor_tensor(bias, k.weight["b_3p"][:, :], k.weight["b_3n"][:, :], ALU.subtract))
        chain.link(v.tensor_tensor(k.h[:, :, :], k.h[:, :, :], over_tiles(bias, NT), ALU.add))
        chain.link(v.scalar_tensor_tensor(k.h[:, :, :], k.h[:, :, :], 0.0, k.x[:, :, :], ALU.max, ALU.add))
        layer_norm(phase, dve, chain, 1)

    phase.after = after
    phase.tables = [(out.rearrange("(t p) f -> p t f", p=P), k.x[:, :, :])]
    phase.build()



INPUTS = {
    "x": [NPAD, D], "src": [P, ET], "dst": [P, ET], "edge_type_8": [P, ET], "edge_weight": [P, ET],
    "edge_attr_64": [D, EPAD], "dst_rows": [ET // 7, 7, P],
}
for layer in range(3):
    INPUTS.update({f"L0_gnn_W{layer}": [D, D], f"L0_gnn_b{layer}": [D], f"L0_gnn_a{layer}": [2, D],
                   f"L0_gnn_ab{layer}": [1]})
INPUTS.update({
    "L1_gnn_u": [16, D], "L1_gnn_W1a": [2 * D, H], "L1_gnn_b1a": [H], "L1_gnn_W1b": [H, D], "L1_gnn_b1b": [D],
    "L1_gnn_W2a": [3 * D, H], "L1_gnn_b2a": [H], "L1_gnn_W2b": [H, D], "L1_gnn_b2b": [D],
    "L2_gnn_weight": [D, RELS * D], "L2_gnn_self_loop_w": [D, D],
    "L3_gnn_W1": [2 * D, H], "L3_gnn_b1p": [H], "L3_gnn_b1n": [H], "L3_gnn_W2": [H, 2 * D],
    "L3_gnn_b2p": [D], "L3_gnn_b2n": [D],
})
INTS = ("src", "dst", "dst_rows", "edge_type_8")


def program(nc, dram, out):
    with ExitStack() as ctx:
        k = Program(nc, ctx, dram)
        scratch = lambda name, rows, cols: nc.dram_tensor(name, (rows, cols), FP32, kind="Internal").ap()
        y_table = scratch("y_table", NPAD, H)
        rel_table, sign_table = scratch("rel_table", NPAD * RELS, D), scratch("sign_table", NPAD * 2, D)
        setup(k)
        att = Attention(k)
        build_counts(k, att)
        for layer in range(3):
            attention_nodes(k, layer, att)
            attention_layer(k, f"a{layer}", att)
        edge_table(k, y_table)
        scatter_pass(k, "ep", y_table, k.src_idx, H, HROW, "edge")
        edge_mean(k)
        node_mlp(k)
        relation_table(k, rel_table)
        scatter_pass(k, "rp", rel_table, k.rel_idx, D, D, "rows")
        signed_table(k, sign_table)
        scatter_pass(k, "sp", sign_table, k.sign_idx, D, H, "signed")
        gcn_mid(k, sign_table)
        scatter_pass(k, "sq", sign_table, k.sign_idx, D, H, "signed")
        gcn_finish(k, out)


def layout(inputs):
    import numpy as np

    def edges(a, pad=0):
        padded = np.full(EPAD, pad, a.dtype)
        padded[:E] = a
        return np.ascontiguousarray(padded.reshape(ET, P).T)

    a = {name: np.asarray(value) for name, value in inputs.items()}
    got = {}
    got["x"] = np.zeros((NPAD, D), a["x"].dtype)
    got["x"][:N] = a["x"]
    for name in ("src", "edge_type_8", "edge_weight"):
        got[name] = edges(a[name])
    got["dst"] = edges(a["dst"], NPAD - 1)
    got["dst_rows"] = np.ascontiguousarray(got["dst"].T).reshape(ET // 7, 7, P)
    got["edge_attr_64"] = np.zeros((D, EPAD), a["edge_attr_64"].dtype)
    got["edge_attr_64"][:, :E] = a["edge_attr_64"].T
    for l in range(3):
        got[f"L0_gnn_W{l}"] = np.ascontiguousarray(a[f"L0_gnn_W{l}"].T)
        got[f"L0_gnn_b{l}"] = a[f"L0_gnn_b{l}"]
        got[f"L0_gnn_a{l}"] = a[f"L0_gnn_a{l}"].reshape(2, D)
        got[f"L0_gnn_ab{l}"] = a[f"L0_gnn_ab{l}"]
    got["L2_gnn_weight"] = np.ascontiguousarray(a["L2_gnn_weight"].transpose(1, 0, 2).reshape(D, RELS * D))
    got["L2_gnn_self_loop_w"] = np.ascontiguousarray(a["L2_gnn_self_loop_w"].T)
    got["L3_gnn_W1"] = np.concatenate([a["L3_gnn_W1p"].T, a["L3_gnn_W1n"].T], axis=0)
    got["L3_gnn_W2"] = np.concatenate([a["L3_gnn_W2p"].T, a["L3_gnn_W2n"].T], axis=1)
    return {name: got.get(name, a.get(name)) for name in INPUTS}


def kernel(**inputs):
    import concourse.bacc as bacc
    from concourse.bass_utils import run_bass_kernel_spmd as run

    nc = bacc.Bacc("TRN2", target_bir_lowering=False, num_devices=1)
    arrays = {"in_" + name: a for name, a in layout(inputs).items()}
    dram = {name: nc.dram_tensor("in_" + name, tuple(shape), INT32 if name in INTS else FP32, kind="ExternalInput").ap()
            for name, shape in INPUTS.items()}
    out = nc.dram_tensor("out", (NPAD, D), FP32, kind="ExternalOutput").ap()
    program(nc, dram, out)
    return run(nc, [arrays], core_ids=[0]).results[0]["out"][:N]
```
